# Optimizing a Trainium2 kernel written in Bass

```python
import numpy as np
import jax
import jax.numpy as jnp

def _softmax(x, axis=-1):
    return jax.nn.softmax(x, axis=axis)

def _gelu(x):
    return jax.nn.gelu(x, approximate=True)

def _silu(x):
    return jax.nn.silu(x)

def _sigmoid(x):
    return jax.nn.sigmoid(x)

def _layernorm(x, axis=-1, eps=1e-05):
    m = jnp.mean(x, axis=axis, keepdims=True)
    v = jnp.var(x, axis=axis, keepdims=True)
    return (x - m) / jnp.sqrt(v + eps)

def _scatter_add(tgt, idx, src, axis=0):
    return tgt.at[idx].add(src)

def _segment_sum(src, seg, n):
    return jax.ops.segment_sum(src, seg, n)
kernel_name = 'mk_adaln_d1_jaxref_r8_a74041'

def setup_inputs(seed: int=0):
    np.random.seed(seed)
    _w = jnp.asarray

    def _L0_attn_setup():
        import jax, jax.numpy as jnp
        import numpy as np
        D_MODEL = 128
        D_STATE = 16
        D_CONV = 4
        EXPAND = 2
        D_INNER = EXPAND * D_MODEL
        DT_RANK = D_MODEL // 16
        B, L = (2, 128)
        EPS = 1e-06

        def _rmsnorm(x, w):
            ss = jnp.sum(x * x, axis=-1, keepdims=True)
            return w * x / jnp.sqrt(ss + EPS)

        def _mamba(x, in_proj_w, conv_w, conv_b, x_proj_w, dt_proj_w, dt_proj_b, A_log, Dp, out_proj_w):
            xz = jnp.einsum('bld,ed->ble', x, in_proj_w)
            xm, z = jnp.split(xz, 2, axis=-1)
            xc = jnp.transpose(xm, (0, 2, 1))
            xc = jax.lax.conv_general_dilated(xc, conv_w, window_strides=(1,), padding=[(D_CONV - 1, 0)], feature_group_count=D_INNER)
            xc = xc + conv_b[None, :, None]
            u = jax.nn.silu(jnp.transpose(xc, (0, 2, 1)))
            dbc = jnp.einsum('bld,ed->ble', u, x_proj_w)
            dt = dbc[..., :DT_RANK]
            Bm = dbc[..., DT_RANK:DT_RANK + D_STATE]
            Cm = dbc[..., DT_RANK + D_STATE:]
            delta = jax.nn.softplus(jnp.einsum('blr,dr->bld', dt, dt_proj_w) + dt_proj_b)
            A = -jnp.exp(A_log)
            dA = jnp.exp(delta[..., None] * A)
            dBu = delta[..., None] * Bm[:, :, None, :] * u[..., None]

            def step(h, inp):
                dA_t, dBu_t, C_t = inp
                h = dA_t * h + dBu_t
                y = jnp.einsum('bdn,bn->bd', h, C_t)
                return (h, y)
            h0 = jnp.zeros((x.shape[0], D_INNER, D_STATE), x.dtype)
            _, ys = jax.lax.scan(step, h0, (dA.swapaxes(0, 1), dBu.swapaxes(0, 1), Cm.swapaxes(0, 1)))
            y = ys.swapaxes(0, 1) + u * Dp
            y = y * jax.nn.silu(z)
            return jnp.einsum('ble,de->bld', y, out_proj_w)
        key = jax.random.key(seed)
        ks = jax.random.split(key, 12)

        def rn(k, shape, scale=0.02):
            return jax.random.normal(k, shape, jnp.float32) * scale
        A_log = jnp.log(jnp.broadcast_to(jnp.arange(1, D_STATE + 1, dtype=jnp.float32), (D_INNER, D_STATE)))
        return {'x': jax.random.normal(ks[0], (B, L, D_MODEL), jnp.float32), 'norm1_w': jnp.ones((D_MODEL,), jnp.float32), 'norm2_w': jnp.ones((D_MODEL,), jnp.float32), 'in_proj_w': rn(ks[1], (2 * D_INNER, D_MODEL)), 'conv_w': rn(ks[2], (D_INNER, 1, D_CONV), 0.1), 'conv_b': jnp.zeros((D_INNER,), jnp.float32), 'x_proj_w': rn(ks[3], (DT_RANK + 2 * D_STATE, D_INNER)), 'dt_proj_w': rn(ks[4], (D_INNER, DT_RANK), 0.1), 'dt_proj_b': rn(ks[5], (D_INNER,), 0.1), 'A_log': A_log, 'D': jnp.ones((D_INNER,), jnp.float32), 'out_proj_w': rn(ks[6], (D_MODEL, D_INNER)), 'mlp_w1': rn(ks[7], (4 * D_MODEL, D_MODEL)), 'mlp_b1': jnp.zeros((4 * D_MODEL,), jnp.float32), 'mlp_w2': rn(ks[8], (D_MODEL, 4 * D_MODEL)), 'mlp_b2': jnp.zeros((D_MODEL,), jnp.float32)}
    _L0_attn_in = _L0_attn_setup()

    def _L0_ffn_setup():
        import math
        import jax, jax.numpy as jnp
        import numpy as np
        B, T, D, N, H = (8, 256, 128, 16, 256)
        CAP_FACTOR = 1.25
        key = jax.random.key(seed)
        ks = jax.random.split(key, 4)
        x = jax.random.normal(ks[0], (B, T, D), jnp.float32)
        Wg = jax.random.normal(ks[1], (D, N), jnp.float32) * D ** (-0.5)
        W1 = jax.random.normal(ks[2], (N, D, H), jnp.float32) * D ** (-0.5)
        b1 = jnp.zeros((N, H), jnp.float32)
        W2 = jax.random.normal(ks[3], (N, H, D), jnp.float32) * H ** (-0.5)
        b2 = jnp.zeros((N, D), jnp.float32)
        return {'x': x, 'Wg': Wg, 'W1': W1, 'b1': b1, 'W2': W2, 'b2': b2}
    _L0_ffn_in = _L0_ffn_setup()
    _L0_c = _w((lambda *s: np.random.randn(*s).astype(np.float32) * 0.05)(8, 128))
    _L0_wmod = _w((lambda *s: np.random.randn(*s).astype(np.float32) * 0.05)(128, 6 * 128) * 128 ** (-0.5))
    _d = {'L0_attn_x': _L0_attn_in['x'], 'L0_attn_norm1_w': _L0_attn_in['norm1_w'], 'L0_attn_norm2_w': _L0_attn_in['norm2_w'], 'L0_attn_in_proj_w': _L0_attn_in['in_proj_w'], 'L0_attn_conv_w': _L0_attn_in['conv_w'], 'L0_attn_conv_b': _L0_attn_in['conv_b'], 'L0_attn_x_proj_w': _L0_attn_in['x_proj_w'], 'L0_attn_dt_proj_w': _L0_attn_in['dt_proj_w'], 'L0_attn_dt_proj_b': _L0_attn_in['dt_proj_b'], 'L0_attn_A_log': _L0_attn_in['A_log'], 'L0_attn_D': _L0_attn_in['D'], 'L0_attn_out_proj_w': _L0_attn_in['out_proj_w'], 'L0_attn_mlp_w1': _L0_attn_in['mlp_w1'], 'L0_attn_mlp_b1': _L0_attn_in['mlp_b1'], 'L0_attn_mlp_w2': _L0_attn_in['mlp_w2'], 'L0_attn_mlp_b2': _L0_attn_in['mlp_b2'], 'L0_ffn_Wg': _L0_ffn_in['Wg'], 'L0_ffn_W1': _L0_ffn_in['W1'], 'L0_ffn_b1': _L0_ffn_in['b1'], 'L0_ffn_W2': _L0_ffn_in['W2'], 'L0_ffn_b2': _L0_ffn_in['b2'], 'L0_c': _L0_c, 'L0_wmod': _L0_wmod}
    _x0 = _d['L0_attn_x']
    _d['L0_attn_x'] = jax.random.normal(jax.random.fold_in(jax.random.key(seed), 1), (8, 256, 128), dtype=_x0.dtype)
    del _x0
    return _d

def reference(L0_attn_x, L0_attn_norm1_w, L0_attn_norm2_w, L0_attn_in_proj_w, L0_attn_conv_w, L0_attn_conv_b, L0_attn_x_proj_w, L0_attn_dt_proj_w, L0_attn_dt_proj_b, L0_attn_A_log, L0_attn_D, L0_attn_out_proj_w, L0_attn_mlp_w1, L0_attn_mlp_b1, L0_attn_mlp_w2, L0_attn_mlp_b2, L0_ffn_Wg, L0_ffn_W1, L0_ffn_b1, L0_ffn_W2, L0_ffn_b2, L0_c, L0_wmod):

    def _L0_attn_ref(x, norm1_w, norm2_w, in_proj_w, conv_w, conv_b, x_proj_w, dt_proj_w, dt_proj_b, A_log, D, out_proj_w, mlp_w1, mlp_b1, mlp_w2, mlp_b2):
        import jax, jax.numpy as jnp
        import numpy as np
        D_MODEL = 128
        D_STATE = 16
        D_CONV = 4
        EXPAND = 2
        D_INNER = EXPAND * D_MODEL
        DT_RANK = D_MODEL // 16
        B, L = (2, 128)
        EPS = 1e-06

        def _rmsnorm(x, w):
            ss = jnp.sum(x * x, axis=-1, keepdims=True)
            return w * x / jnp.sqrt(ss + EPS)

        def _mamba(x, in_proj_w, conv_w, conv_b, x_proj_w, dt_proj_w, dt_proj_b, A_log, Dp, out_proj_w):
            xz = jnp.einsum('bld,ed->ble', x, in_proj_w)
            xm, z = jnp.split(xz, 2, axis=-1)
            xc = jnp.transpose(xm, (0, 2, 1))
            xc = jax.lax.conv_general_dilated(xc, conv_w, window_strides=(1,), padding=[(D_CONV - 1, 0)], feature_group_count=D_INNER)
            xc = xc + conv_b[None, :, None]
            u = jax.nn.silu(jnp.transpose(xc, (0, 2, 1)))
            dbc = jnp.einsum('bld,ed->ble', u, x_proj_w)
            dt = dbc[..., :DT_RANK]
            Bm = dbc[..., DT_RANK:DT_RANK + D_STATE]
            Cm = dbc[..., DT_RANK + D_STATE:]
            delta = jax.nn.softplus(jnp.einsum('blr,dr->bld', dt, dt_proj_w) + dt_proj_b)
            A = -jnp.exp(A_log)
            dA = jnp.exp(delta[..., None] * A)
            dBu = delta[..., None] * Bm[:, :, None, :] * u[..., None]

            def step(h, inp):
                dA_t, dBu_t, C_t = inp
                h = dA_t * h + dBu_t
                y = jnp.einsum('bdn,bn->bd', h, C_t)
                return (h, y)
            h0 = jnp.zeros((x.shape[0], D_INNER, D_STATE), x.dtype)
            _, ys = jax.lax.scan(step, h0, (dA.swapaxes(0, 1), dBu.swapaxes(0, 1), Cm.swapaxes(0, 1)))
            y = ys.swapaxes(0, 1) + u * Dp
            y = y * jax.nn.silu(z)
            return jnp.einsum('ble,de->bld', y, out_proj_w)
        h = x + _mamba(_rmsnorm(x, norm1_w), in_proj_w, conv_w, conv_b, x_proj_w, dt_proj_w, dt_proj_b, A_log, D, out_proj_w)
        hn = _rmsnorm(h, norm2_w)
        m = jax.nn.gelu(jnp.einsum('bld,fd->blf', hn, mlp_w1) + mlp_b1, approximate=False)
        m = jnp.einsum('blf,df->bld', m, mlp_w2) + mlp_b2
        return h + m

    def _L0_ffn_ref(x, Wg, W1, b1, W2, b2):
        import math
        import jax, jax.numpy as jnp
        import numpy as np
        B, T, D, N, H = (8, 256, 128, 16, 256)
        CAP_FACTOR = 1.25
        b, t, d = x.shape
        n = Wg.shape[1]
        bt = b * t
        cap = math.ceil(CAP_FACTOR * bt / n)
        logits = jnp.einsum('btd,dn->btn', x, Wg)
        probs = jax.nn.softmax(logits, axis=-1)
        top1_val = probs.max(axis=-1).reshape(bt)
        top1_idx = probs.argmax(axis=-1).reshape(bt)
        x_flat = x.reshape(bt, d)
        masked = jnp.where(top1_idx[None, :] == jnp.arange(n)[:, None], top1_val[None, :], -jnp.inf)
        vals, idx = jax.lax.top_k(masked, cap)
        valid = jnp.isfinite(vals)
        xe = x_flat[idx]
        h = jax.nn.gelu(jnp.einsum('ncd,ndh->nch', xe, W1) + b1[:, None, :])
        out = jnp.einsum('nch,nhd->ncd', h, W2) + b2[:, None, :]
        safe_idx = jnp.where(valid, idx, bt)
        y_flat = x_flat.at[safe_idx.reshape(-1)].set(out.reshape(-1, d), mode='drop')
        return y_flat.reshape(b, t, d)
    x = L0_attn_x
    mod = (_silu(L0_c) @ L0_wmod).reshape(L0_c.shape[0], 6, 1, -1)
    sa, ca, ga, sb, cb, gb = (mod[:, 0], mod[:, 1], mod[:, 2], mod[:, 3], mod[:, 4], mod[:, 5])
    ga = (2 * (ga >= 0) - 1) * jnp.maximum(jnp.abs(ga), 0.25)
    gb = (2 * (gb >= 0) - 1) * jnp.maximum(jnp.abs(gb), 0.25)
    h = _layernorm(x, axis=-1) * (1 + ca) + sa
    x = x + ga * _L0_attn_ref(h, L0_attn_norm1_w, L0_attn_norm2_w, L0_attn_in_proj_w, L0_attn_conv_w, L0_attn_conv_b, L0_attn_x_proj_w, L0_attn_dt_proj_w, L0_attn_dt_proj_b, L0_attn_A_log, L0_attn_D, L0_attn_out_proj_w, L0_attn_mlp_w1, L0_attn_mlp_b1, L0_attn_mlp_w2, L0_attn_mlp_b2)
    h = _layernorm(x, axis=-1) * (1 + cb) + sb
    x = x + gb * _L0_ffn_ref(h, L0_ffn_Wg, L0_ffn_W1, L0_ffn_b1, L0_ffn_W2, L0_ffn_b2)
    return x

_drawn_inputs = setup_inputs


def setup_inputs(seed=0):
    import zlib

    import numpy as np

    out = dict(_drawn_inputs(seed))
    spreads = {'L0_attn_norm1_w': (1.0, 0.6),
     'L0_attn_norm2_w': (1.0, 0.6),
     'L0_attn_conv_b': (0.0, 0.8),
     'L0_attn_D': (1.0, 0.6),
     'L0_attn_mlp_b1': (0.0, 0.499),
     'L0_attn_mlp_b2': (0.0, 0.1),
     'L0_ffn_b1': (0.0, 0.491),
     'L0_ffn_b2': (0.0, 0.329)}
    factors = {'L0_attn_in_proj_w': 8.0,
     'L0_attn_conv_w': 8.0,
     'L0_attn_x_proj_w': 8.0,
     'L0_attn_dt_proj_w': 8.0,
     'L0_attn_dt_proj_b': 8.0,
     'L0_attn_A_log': 8.0,
     'L0_attn_out_proj_w': 8.0,
     'L0_attn_mlp_w1': 8.0,
     'L0_attn_mlp_w2': 3.405}
    for name, (base, spread) in spreads.items():
        noise = np.random.default_rng([zlib.crc32(name.encode()), seed]).standard_normal(out[name].shape)
        drawn = base * np.exp(spread * noise) if base else spread * noise
        out[name] = jnp.asarray(drawn.astype(out[name].dtype))
    for name, factor in factors.items():
        out[name] = (out[name] * factor).astype(out[name].dtype)
    return out
```

```python
from contextlib import ExitStack

import concourse.bass as bass
from concourse import mybir

F32 = mybir.dt.float32
BF16 = mybir.dt.bfloat16
U32 = mybir.dt.uint32
ALU = mybir.AluOpType
ACT = mybir.ActivationFunctionType
AX_X = mybir.AxisListType.X

P = 128
NB, T = 8, 256
D = 128
DI = 2 * D
NH = DI // P
NS = 16
RANK = D // 16
TAPS = 4
F = 4 * D
FB = F // P
TOK = NB * T
NT = TOK // P
CH = 512
NC = TOK // CH
TC = CH // P
BC = CH // T
NE, H = 16, 256
CAP = -(-5 * TOK // (4 * NE))
SLOTS = NE * CAP
ST = SLOTS // P
G = RANK + 2 * NS
PARTS = 3
W_PAY = 3 * D + 1
SA, CA, GA, SB, CB, GB = range(6)
FAR = 8192.0
STEPS = NS


def adaln_mamba_moe(nc, a, out, xe_dram, dbg):
    with ExitStack() as ctx:
        def sb(name, shape, dt=F32):
            return ctx.enter_context(nc.sbuf_tensor(name, shape, dt))

        def sem(name):
            return ctx.enter_context(nc.semaphore(name))

        x = sb("x", [P, NT, D])
        w_in = sb("w_in", [D, 2 * DI])
        w_xp = sb("w_xp", [P, NH, PARTS * G])
        w_dt = sb("w_dt", [RANK, DI])
        w_out = sb("w_out", [P, NH, D])
        w_m1 = sb("w_m1", [D, F])
        w_m2 = sb("w_m2", [P, FB, D])
        w_g = sb("w_g", [D, NE])
        w_e1 = sb("w_e1", [D, NE, H])
        w_e2 = sb("w_e2", [P, NE, H // P, D])
        chan = sb("chan", [P, NH, TAPS + 3 + NS])
        cols = sb("cols", [P, 2 + FB + 2 * NE + NE])
        b2row = sb("b2row", [1, D])
        c_t = sb("c_t", [D, PARTS * NB])
        w_mod = sb("w_mod", [D, 6 * D])
        consts = sb("consts", [P, 3 * P + 2 * NS + 64])
        ident = consts[:, 0:P]
        earlier = consts[:, P:2 * P]
        token1 = consts[:, 2 * P:2 * P + NT]
        prefer = consts[:, 2 * P + NT:2 * P + NT + NE]
        o_ = 2 * P + NT + NE
        sel_rows = consts[0:PARTS * G, o_:o_ + 2 * NS]
        o_ += 2 * NS
        sel_batch = consts[0:PARTS * NB, o_:o_ + NB]
        o_ += NB
        cut_g = consts[0:PARTS * G, o_:o_ + 2]
        cut_m = consts[0:PARTS * NB, o_ + 2:o_ + 4]
        half = consts[:, o_ + 4:o_ + 4 + TC]
        ones = sb("ones", [1, P])
        id16 = sb("id16", [P, P], BF16)
        sel = sb("sel", [PARTS * G, 2 * NS, P], BF16)
        bsel = sb("bsel", [PARTS * NB, NB, P], BF16)
        neg_a = sb("neg_a", [P, NH, NS])

        silu_c = sb("silu_c", [D, PARTS * NB])
        mod = sb("mod", [PARTS * NB, 6 * D])
        mod_hi = sb("mod_hi", [PARTS * NB, 6 * D], BF16)
        mod_t = sb("mod_t", [PARTS * NB, 6 * D])
        mod_parts = sb("mod_parts", [PARTS * NB, 6 * D], BF16)
        mod_b = sb("mod_b", [P, NB, 5 * D])

        bn = sb("bn", [P, TC, 6])
        mv = sb("mv", [P, TC, 2])
        ss = sb("ss", [P, TC])
        rs = sb("rs", [P, TC])

        h = sb("h", [P, TC, D])
        hn = sb("hn", [P, TC, D])
        h_t = sb("h_t", [D, CH])
        pay = sb("pay", [P, NT, W_PAY])
        base = sb("base", [P, TC, D])
        logits = sb("logits", [P, NT, NE])

        arena = sb("arena", [P, 16384])
        at = [0]

        def take(n):
            at[0] += n
            assert at[0] <= 16384, at[0]
            return arena[:, at[0] - n:at[0]]

        u = take(NH * CH).rearrange("p (h t) -> p h t", h=NH)
        zg = take(NH * CH).rearrange("p (h t) -> p h t", h=NH)
        delta = take(NH * CH).rearrange("p (h t) -> p h t", h=NH)
        du = take(NH * CH).rearrange("p (h t) -> p h t", h=NH)
        soft = take(NH * CH).rearrange("p (h t) -> p h t", h=NH)
        b_rows = take(2 * CH).rearrange("p (k t) -> p k t", k=2)
        drive = take(2 * NH * CH).rearrange("p (k t) -> p k t", k=2)
        state = take(2 * NH * CH).rearrange("p (k t) -> p k t", k=2)
        part = take(2 * NH * CH).rearrange("p (k t) -> p k t", k=2)
        m_t = take(FB * CH).rearrange("p (f t) -> p f t", f=FB)
        at[0] = 0
        xe = take(ST * W_PAY).rearrange("p (s w) -> p s w", w=W_PAY)
        xe_t = take(SLOTS)
        o_t = take(SLOTS)
        fin = take(SLOTS).rearrange("p (s d) -> p s d", d=D)
        g_t = take(2 * 2 * CAP).rearrange("p (k h s) -> p k h s", k=2, h=2)
        dbc_hi = sb("dbc_hi", [PARTS * G, CH], BF16)
        dbc_t = sb("dbc_t", [PARTS * G, CH])
        dbc_parts = sb("dbc_parts", [PARTS * G, CH], BF16)
        dt_rows = sb("dt_rows", [RANK, CH])

        at[0] = 0
        sm = take(NT * NE).rearrange("p (t e) -> p t e", e=NE)
        hot = take(NT * NE).rearrange("p (t e) -> p t e", e=NE)
        msk = take(NT * NE).rearrange("p (t e) -> p t e", e=NE)
        msk_r = take(NT * NE).rearrange("p (t e) -> p t e", e=NE)
        m_parts = take(NT * PARTS * NE // 2).bitcast(BF16).rearrange("p (t k e) -> p t k e", k=PARTS, e=NE)
        h_parts = take(NT * PARTS * NE // 2).bitcast(BF16).rearrange("p (t k e) -> p t k e", k=PARTS, e=NE)
        m_rows = take(TOK // 2)[0:PARTS * NE, :].bitcast(BF16)
        h_rows = take(TOK // 2)[0:PARTS * NE, :].bitcast(BF16)
        junk = take(TOK).bitcast(BF16).rearrange("p (k t) -> p k t", k=2)
        junk2 = take(2 * P).rearrange("p (k t) -> p k t", k=2)
        top = sb("top", [P, NT])
        first = sb("first", [P, NT])
        cnt = sb("cnt", [P, NT, 3])
        slot_f = sb("slot_f", [P, NT, 4])
        slot = sb("slot", [P, NT], U32)
        tok_f = sb("tok_f", [P, ST, 2])
        tok = sb("tok", [P, ST], U32)
        zeros = m_t.rearrange("p f t -> p (f t)")[:, 0:4 * W_PAY]

        ps = ctx.enter_context(nc.psum_tensor("ps", [P, 8, CH], F32))
        bank_b, bank_c = ps[:, 0, :], ps[:, 1, :]
        decay = ps[:, 2:4, :]
        ysum = ps[:, 4:6, :]
        side = [ps[:, 6, :], ps[:, 7, :]]

        block = ctx.enter_context(nc.Block())
        S = {n: sem(n) for n in (
            "ld_mod", "ld_const", "ld_w", "ld_m", "ld_e", "dram_zeroed", "base_out", "rows_out", "xe_in", "rg_in", "final_out",
            "silu_c_ok", "mod_mm", "mod_raw", "mod_hi_ok", "mod_parts_ok", "mod_bc", "mod_bc_copied", "mod_bc_copied_v",
            "gate_rows", "sel_ok", "decay_zeroed", "neg_a_ok",
            "ln_var", "ln_rstd", "rms_ss", "rms_rs", "hn_ok", "hn_tr", "h_t_ok",
            "xm_mm", "conv0", "conv_ok", "u_ok", "z_mm", "z_ok", "dbc_mm", "dbc_copied", "dbc_r1", "dbc_mid", "dbc_ok",
            "dt_ok", "dp_mm", "dp_abs", "dp_max", "dp_ln", "delta_ok", "du_ok",
            "b_bcast", "b_copied", "drive_ok", "decay_ok", "scanned", "c_bcast", "weighted", "summed",
            "y_read", "yg_ok", "op_mm", "h2_ok", "rms2_ss", "rms2_rs", "hn2_ok", "hn2_tr", "h2_t_ok", "f1_mm", "gelu_ok",
            "f2_mm", "f2_read", "ln2_var", "ln2_rstd", "hm_ok", "hm_tr", "hm_t_ok", "lg_mm", "lg_ok", "base_ok", "x1_ok",
            "e_exp", "e_d", "parts_ok", "hid_ok", "rt_tr", "rt_rows", "row_mm", "ranked", "slot_ok", "zero_ok",
            "xt_tr", "xt_ok", "e1_mm", "e1_ok", "e2_mm", "e2_ok", "o_tr", "fin_ok", "tok_ok",
            "dve_step", "act_step", "pool_step")}
        S["ld_x"] = [sem(f"ld_x{c}") for c in range(NC)]

        def chunk(c):
            return slice(TC * c, TC * (c + 1))

        @block.sync
        def _(sp):
            sp.dma_start(c_t[:], a["c_t"]).then_inc(S["ld_mod"], 16)
            sp.dma_start(w_mod[:], a["w_mod"]).then_inc(S["ld_mod"], 16)
            sp.dma_start(consts[:], a["consts"]).then_inc(S["ld_const"], 16)
            for c in range(NC):
                sp.dma_start(x[:, chunk(c), :], a["x"][:, chunk(c), :]).then_inc(S["ld_x"][c], 16)
                if c == 0:
                    sp.dma_start(cols[:], a["cols"]).then_inc(S["ld_w"], 16)
                    sp.dma_start(chan[:], a["chan"]).then_inc(S["ld_w"], 16)
                    sp.dma_start(w_in[:], a["w_in"]).then_inc(S["ld_w"], 16)
                    sp.dma_start(w_xp[:], a["w_xp"]).then_inc(S["ld_w"], 16)
                    sp.dma_start(w_dt[:], a["w_dt"]).then_inc(S["ld_w"], 16)
            sp.dma_start(w_out[:], a["w_out"]).then_inc(S["ld_m"], 16)
            sp.dma_start(w_m1[:], a["w_m1"]).then_inc(S["ld_m"], 16)
            sp.dma_start(w_m2[:], a["w_m2"]).then_inc(S["ld_m"], 16)
            sp.dma_start(b2row[:], a["b2row"]).then_inc(S["ld_m"], 16)
            sp.dma_start(w_g[:], a["w_g"]).then_inc(S["ld_m"], 16)
            sp.wait_ge(S["zero_ok"], 1)
            rows = xe_dram.rearrange("(p s) w -> p (s w)", p=P)
            for s in range(0, ST, 4):
                sp.dma_start(rows[:, s * W_PAY:(s + 4) * W_PAY], zeros).then_inc(S["dram_zeroed"], 16)
            sp.dma_start(w_e1[:], a["w_e1"]).then_inc(S["ld_e"], 16)
            sp.dma_start(w_e2[:], a["w_e2"]).then_inc(S["ld_e"], 16)
            ov = out.rearrange("b (t p) d -> p (b t) d", p=P)
            for c in range(NC):
                sp.wait_ge(S["base_ok"], c + 1)
                sp.dma_start(ov[:, chunk(c), :], base[:]).then_inc(S["base_out"], 16)
            sp.wait_ge(S["rows_out"], 16 * NT)
            xv = xe_dram.rearrange("(s p) w -> p s w", p=P)
            for s in range(0, ST, 4):
                sp.dma_start(xe[:, s:s + 4, :], xv[:, s:s + 4, :]).then_inc(S["xe_in"], 16)
            sp.wait_ge(S["base_out"], 16 * NC)
            sp.wait_ge(S["final_out"], 16 * ST)

        @block.gpsimd
        def _(gp):
            n_step = [0]

            def step(ins):
                n_step[0] += 1
                ins.then_inc(S["pool_step"], 1)

            def settle():
                gp.wait_ge(S["pool_step"], n_step[0])

            nc.gpsimd.memset(zeros, 0.0).then_inc(S["zero_ok"], 1)
            nc.gpsimd.memset(ones[:], 1.0).then_inc(S["sel_ok"], 1)
            gp.wait_ge(S["ld_const"], 16)
            step(nc.gpsimd.tensor_copy(pay[:, :, 3 * D], token1))

            def inverse_root(src, eps, done, ready, c, count=1):
                gp.wait_ge(ready, c + 1)
                step(nc.gpsimd.tensor_scalar(rs[:], src, eps, None, ALU.add))
                settle()
                nc.gpsimd.tensor_tensor(rs[:], rs[:], half, ALU.pow).then_inc(done, 1)

            def front(c):
                inverse_root(mv[:, :, 1], 1e-5, S["ln_rstd"], S["ln_var"], c)
                inverse_root(ss[:], 1e-6, S["rms_rs"], S["rms_ss"], c)
                gp.wait_ge(S["dp_ln"], 2 * (c + 1))
                gp.wait_ge(S["dp_max"], 2 * (c + 1))
                gp.wait_ge(S["u_ok"], 2 * (c + 1))
                nc.gpsimd.tensor_tensor(delta, delta, soft, ALU.add).then_inc(S["delta_ok"], 1)
                gp.wait_ge(S["delta_ok"], c + 1)
                nc.gpsimd.tensor_tensor(du, delta, u, ALU.mult).then_inc(S["du_ok"], 1)
                gp.wait_ge(S["du_ok"], c + 1)

            def drive_step(k, n, buf):
                gp.wait_ge(S["b_copied"], k + n + 1)
                if not (isinstance(n, int) and k + n < 2):
                    gp.wait_ge(S["scanned"], 2 * (k + n - 1))
                nc.gpsimd.tensor_tensor(
                    drive[:, buf, :].rearrange("p (h t) -> p h t", h=NH), du,
                    b_rows[:, buf, :].unsqueeze(1).to_broadcast([P, NH, CH]), ALU.mult).then_inc(S["drive_ok"], 1)

            def scan(c):
                k = STEPS * c
                drive_step(k, 0, 0)
                drive_step(k, 1, 1)
                with gp.Fori(1, STEPS // 2) as i:
                    drive_step(k, i * 2, 0)
                    drive_step(k, i * 2 + 1, 1)

            def back(c):
                gp.wait_ge(S["y_read"], c + 1)
                nc.gpsimd.tensor_tensor(u, u, zg, ALU.mult).then_inc(S["yg_ok"], 1)
                inverse_root(ss[:], 1e-6, S["rms2_rs"], S["rms2_ss"], c)
                inverse_root(mv[:, :, 1], 1e-5, S["ln2_rstd"], S["ln2_var"], c)
                gp.wait_ge(S["hm_ok"], c + 1)
                gp.wait_ge(S["gate_rows"], NB)
                if c:
                    gp.wait_ge(S["base_out"], 16 * c)
                t = pay[:, chunk(c), :]
                step(nc.gpsimd.tensor_tensor(base[:], t[:, :, 0:D], t[:, :, 2 * D:3 * D], ALU.mult))
                settle()
                nc.gpsimd.tensor_tensor(base[:], base[:], t[:, :, D:2 * D], ALU.add).then_inc(S["base_ok"], 1)

            for c in range(NC):
                front(c)
                scan(c)
                back(c)

            gp.wait_ge(S["dram_zeroed"], 16 * (ST // 4))
            for t in range(NT):
                gp.wait_ge(S["ranked"], t + 1)
                s = slot_f[:, t, :]
                step(nc.gpsimd.tensor_tensor(s[:, 0:1], cnt[:, t, 0:1], cnt[:, t, 1:2], ALU.add))
                settle()
                step(nc.gpsimd.tensor_tensor(s[:, 1:2], s[:, 0:1], cnt[:, t, 2:3], ALU.add))
                settle()
                step(nc.gpsimd.tensor_scalar(s[:, 2:3], s[:, 1:2], float(CAP), FAR, ALU.is_ge, ALU.mult))
                step(nc.gpsimd.tensor_tensor(s[:, 3:4], s[:, 1:2], first[:, t:t + 1], ALU.add))
                settle()
                nc.gpsimd.tensor_tensor(slot_f[:, t, 0:1], s[:, 2:3], s[:, 3:4], ALU.add).then_inc(S["slot_ok"], 1)
                gp.wait_ge(S["slot_ok"], 2 * t + 1)
                nc.gpsimd.tensor_copy(slot[:, t:t + 1], slot_f[:, t, 0:1]).then_inc(S["slot_ok"], 1)
                gp.wait_ge(S["slot_ok"], 2 * t + 2)
                nc.gpsimd.indirect_dma_start(
                    xe_dram, bass.IndirectOffsetOnAxis(ap=slot[:, t:t + 1], axis=0), pay[:, t, :], None,
                    bounds_check=SLOTS - 1, oob_is_err=False).then_inc(S["rows_out"], 16)

            gp.wait_ge(S["xe_in"], 16 * (ST // 4))
            step(nc.gpsimd.tensor_scalar(tok_f[:, :, 0], xe[:, :, 3 * D], 0.0, FAR, ALU.is_equal, ALU.mult))
            step(nc.gpsimd.tensor_scalar(tok_f[:, :, 1], xe[:, :, 3 * D], -1.0, None, ALU.add))
            settle()
            step(nc.gpsimd.tensor_tensor(tok_f[:, :, 0], tok_f[:, :, 0], tok_f[:, :, 1], ALU.add))
            settle()
            step(nc.gpsimd.tensor_copy(tok[:], tok_f[:, :, 0]))
            settle()
            gp.wait_ge(S["base_out"], 16 * NC)
            flat = out.rearrange("b t d -> (b t) d")
            for s in range(ST):
                gp.wait_ge(S["fin_ok"], s // 4 + 1)
                nc.gpsimd.indirect_dma_start(
                    flat, bass.IndirectOffsetOnAxis(ap=tok[:, s:s + 1], axis=0), fin[:, s, :], None,
                    bounds_check=TOK - 1, oob_is_err=False).then_inc(S["final_out"], 16)

        @block.scalar
        def _(act):
            act.wait_ge(S["ld_mod"], 32)
            nc.scalar.activation(silu_c[:], c_t[:], ACT.Silu).then_inc(S["silu_c_ok"], 1)
            act.wait_ge(S["mod_mm"], 2)
            nc.scalar.activation(mod[:, 0:CH], side[0][0:PARTS * NB, :], ACT.Copy).then_inc(S["mod_raw"], 1)
            nc.scalar.activation(mod[:, CH:6 * D], side[1][0:PARTS * NB, 0:6 * D - CH], ACT.Copy).then_inc(S["mod_raw"], 1)
            act.wait_ge(S["ld_w"], 16 * 5)
            nc.scalar.activation(neg_a[:], chan[:, :, TAPS + 3:], ACT.Exp).then_inc(S["act_step"], 1)
            for b in range(0, NB, 1):
                act.wait_ge(S["mod_bc"], 2 * b + 2)
                nc.scalar.activation(mod_b[:, b, 0:CH], side[0], ACT.Copy).then_inc(S["mod_bc_copied"], 1)
                nc.scalar.activation(mod_b[:, b, CH:5 * D], side[1][:, 0:D], ACT.Copy).then_inc(S["mod_bc_copied"], 1)

            def front(c):
                act.wait_ge(S["hn_tr"], c + 1)
                nc.scalar.activation(h_t[:], side[0], ACT.Copy, scale=cols[:, 0:1]).then_inc(S["h_t_ok"], 1)
                for j in range(NH):
                    act.wait_ge(S["xm_mm"], NH * c + j + 1)
                    nc.scalar.activation(u[:, j, :], side[1 - j], ACT.Identity, bias=chan[:, j, TAPS:TAPS + 1],
                                         scale=chan[:, j, TAPS - 1:TAPS]).then_inc(S["conv0"], 1)
                for j in range(NH):
                    act.wait_ge(S["conv_ok"], NH * c + j + 1)
                    nc.scalar.activation(u[:, j, :], u[:, j, :], ACT.Silu).then_inc(S["u_ok"], 1)
                for j in range(NH):
                    act.wait_ge(S["z_mm"], NH * c + j + 1)
                    nc.scalar.activation(zg[:, j, :], side[1 - j], ACT.Silu).then_inc(S["z_ok"], 1)
                act.wait_ge(S["dbc_mm"], c + 1)
                nc.scalar.activation(dbc_hi[:], side[1][0:PARTS * G, :], ACT.Copy).then_inc(S["dbc_copied"], 1)
                nc.scalar.activation(dt_rows[:], side[1][0:RANK, :], ACT.Copy).then_inc(S["dt_ok"], 1)
                act.wait_ge(S["dbc_r1"], c + 1)
                nc.scalar.activation(dbc_hi[:], dbc_t[:], ACT.Copy).then_inc(S["dbc_mid"], 1)
                for j in range(NH):
                    act.wait_ge(S["dp_mm"], NH * c + j + 1)
                    act.wait_ge(S["dp_max"], NH * c + j + 1)
                    nc.scalar.activation(soft[:, j, :], side[j], ACT.Abs, bias=chan[:, j, TAPS + 1:TAPS + 2]
                                         ).then_inc(S["dp_abs"], 1)
                act.wait_ge(S["dp_abs"], NH * (c + 1))
                nc.scalar.activation(soft, soft, ACT.Exp, scale=-1.0).then_inc(S["act_step"], 1)
                act.wait_ge(S["act_step"], c + 2)
                nc.scalar.activation(soft, soft, ACT.Ln, bias=1.0).then_inc(S["dp_ln"], 2)

            def copy_b(k, n, buf):
                act.wait_ge(S["b_bcast"], k + n + 1)
                if not (isinstance(n, int) and k + n < 2):
                    act.wait_ge(S["drive_ok"], k + n - 1)
                nc.scalar.activation(b_rows[:, buf, :], bank_b, ACT.Copy).then_inc(S["b_copied"], 1)

            def decay_step(k, n):
                for j in range(NH):
                    if not (isinstance(n, int) and k + n < 1):
                        act.wait_ge(S["scanned"], 2 * (k + n - 1) + j + 1)
                    nc.scalar.activation(decay[:, j, :].rearrange("p (b t) -> p b t", b=BC)[:, :, 1:T],
                                         delta[:, j, :].rearrange("p (b t) -> p b t", b=BC)[:, :, 1:T], ACT.Exp,
                                         scale=neg_a[:, j, bass.ds(n, 1)]).then_inc(S["decay_ok"], 1)

            def scan(c):
                k = STEPS * c
                if c == 0:
                    act.wait_ge(S["neg_a_ok"], 1)
                    act.wait_ge(S["decay_zeroed"], 1)
                act.wait_ge(S["delta_ok"], c + 1)
                copy_b(k, 0, 0)
                copy_b(k, 1, 1)
                decay_step(k, 0)
                copy_b(k, 2, 0)
                decay_step(k, 1)
                copy_b(k, 3, 1)
                with act.Fori(1, STEPS // 2 - 1) as i:
                    decay_step(k, i * 2)
                    copy_b(k, i * 2 + 2, 0)
                    decay_step(k, i * 2 + 1)
                    copy_b(k, i * 2 + 3, 1)
                decay_step(k, STEPS - 2)
                decay_step(k, STEPS - 1)

            def back(c):
                act.wait_ge(S["hn2_tr"], c + 1)
                nc.scalar.activation(h_t[:], side[1], ACT.Copy, scale=cols[:, 1:2]).then_inc(S["h2_t_ok"], 1)
                if c == 0:
                    act.wait_ge(S["dram_zeroed"], 16 * (ST // 4))
                for f in range(FB):
                    act.wait_ge(S["f1_mm"], FB * c + f + 1)
                    nc.scalar.activation(m_t[:, f, :], side[f % 2], ACT.Gelu, bias=cols[:, 2 + f:3 + f]
                                         ).then_inc(S["gelu_ok"], 1)
                act.wait_ge(S["hm_tr"], c + 1)
                nc.scalar.activation(h_t[:], side[1], ACT.Copy).then_inc(S["hm_t_ok"], 1)

            for c in range(NC):
                front(c)
                scan(c)
                back(c)

            act.wait_ge(S["e_d"], 1)
            nc.scalar.activation(msk, sm, ACT.Exp).then_inc(S["e_exp"], 1)
            act.wait_ge(S["rt_tr"], 2 * NT)
            nc.scalar.activation(h_rows, ps[0:PARTS * NE, 2:4, :].bitcast(BF16), ACT.Copy).then_inc(S["rt_rows"], 1)
            for e in range(NE):
                act.wait_ge(S["e1_mm"], e + 1)
                if e >= 2:
                    act.wait_ge(S["e2_mm"], e - 1)
                for j in range(2):
                    nc.scalar.activation(g_t[:, e % 2, j, :], ps[:, 2 + e % 2, j * CAP:(j + 1) * CAP], ACT.Gelu_apprx_tanh,
                                         bias=cols[:, 2 + FB + 2 * e + j:3 + FB + 2 * e + j]).then_inc(S["e1_ok"], 1)

        @block.vector
        def _(dve):
            n_step = [0]

            def step(ins):
                n_step[0] += 1
                ins.then_inc(S["dve_step"], 1)

            def settle():
                dve.wait_ge(S["dve_step"], n_step[0])

            v = nc.vector
            step(v.memset(decay.rearrange("p h (b t) -> p (h b) t", t=T)[:, :, 0:1], 0.0))
            dve.wait_ge(S["ld_const"], 16)
            step(v.tensor_copy(id16[:], ident))
            step(v.tensor_copy(bsel[:], sel_batch.unsqueeze(2).to_broadcast([PARTS * NB, NB, P])))
            v.tensor_copy(sel[:], sel_rows.unsqueeze(2).to_broadcast([PARTS * G, 2 * NS, P])).then_inc(S["decay_zeroed"], 1)

            dve.wait_ge(S["mod_raw"], 2)
            m6 = mod[:].rearrange("p (k s d) -> p k s d", k=2, s=3)
            t6 = mod_t[:].rearrange("p (k s d) -> p k s d", k=2, s=3)
            step(v.tensor_scalar(m6[:, :, 1, :], m6[:, :, 1, :], 1.0, None, ALU.add))
            step(v.tensor_scalar(t6[:, :, 0, :], m6[:, :, 2, :], 0.0, 2.0, ALU.is_ge, ALU.mult))
            step(v.scalar_tensor_tensor(t6[:, :, 1, :], m6[:, :, 2, :], -1.0, m6[:, :, 2, :], ALU.mult, ALU.max))
            settle()
            step(v.tensor_scalar(t6[:, :, 1, :], t6[:, :, 1, :], 0.25, None, ALU.max))
            settle()
            step(v.scalar_tensor_tensor(m6[:, :, 2, :], t6[:, :, 0, :], -1.0, t6[:, :, 1, :], ALU.add, ALU.mult))
            settle()
            step(v.tensor_copy(mod_hi[:], mod[:]))
            settle()
            step(v.scalar_tensor_tensor(mod_t[:], mod_hi[:], cut_m[:, 0:1], mod[:], ALU.mult, ALU.add))
            settle()
            step(v.tensor_copy(mod_hi[:], mod_t[:]))
            settle()
            v.scalar_tensor_tensor(mod_parts[:], mod_hi[:], cut_m[:, 1:2], mod_t[:], ALU.mult, ALU.add
                                   ).then_inc(S["mod_parts_ok"], 1)
            dve.wait_ge(S["act_step"], 1)
            v.tensor_scalar(neg_a[:], neg_a[:], -1.0, None, ALU.mult).then_inc(S["neg_a_ok"], 1)
            for b in range(NB):
                dve.wait_ge(S["mod_bc_copied"], 2 * b + 2)
                v.tensor_copy(pay[:, 2 * b:2 * b + 2, 2 * D:3 * D],
                              side[1][:, D:2 * D].unsqueeze(1).to_broadcast([P, 2, D])).then_inc(S["gate_rows"], 1)

            def rows_of(c, section):
                r = mod_b[:, BC * c:BC * (c + 1), section * D:(section + 1) * D]
                return r.unsqueeze(2).to_broadcast([P, BC, TC // BC, D])

            def by_batch(t):
                return t.rearrange("p (b k) d -> p b k d", b=BC)

            def norm(src, var_ready, rstd_ready, c, dst):
                for t in range(TC):
                    step(v.bn_stats(bn[:, t, :], src[:, t, :]))
                settle()
                for t in range(TC):
                    ins = v.bn_aggr(mv[:, t, :], bn[:, t, :])
                    if t < TC - 1:
                        step(ins)
                ins.then_inc(var_ready, 1)
                dve.wait_ge(var_ready, c + 1)
                dve.wait_ge(rstd_ready, c + 1)
                for t in range(TC):
                    step(v.tensor_scalar(dst[:, t, :], src[:, t, :], mv[:, t, 0:1], rs[:, t:t + 1],
                                         ALU.subtract, ALU.mult))
                settle()

            def rms(c, ss_ready, rs_ready, done):
                for t in range(TC):
                    ins = v.scalar_tensor_tensor(hn[:, t, :], h[:, t, :], 1.0, h[:, t, :], ALU.mult, ALU.mult,
                                                 accum_out=ss[:, t:t + 1])
                    if t < TC - 1:
                        step(ins)
                ins.then_inc(ss_ready, 1)
                dve.wait_ge(rs_ready, c + 1)
                for t in range(TC):
                    ins = v.tensor_scalar(hn[:, t, :], h[:, t, :], rs[:, t:t + 1], None, ALU.mult)
                    if t < TC - 1:
                        step(ins)
                ins.then_inc(done, 1)

            def front(c):
                dve.wait_ge(S["ld_x"][c], 16)
                norm(x[:, chunk(c), :], S["ln_var"], S["ln_rstd"], c, h[:])
                dve.wait_ge(S["mod_bc_copied"], 2 * NB)
                step(v.tensor_tensor(by_batch(h[:]), by_batch(h[:]), rows_of(c, CA), ALU.mult))
                settle()
                step(v.tensor_tensor(by_batch(h[:]), by_batch(h[:]), rows_of(c, SA), ALU.add))
                settle()
                if c:
                    dve.wait_ge(S["hn2_tr"], c)
                rms(c, S["rms_ss"], S["rms_rs"], S["hn_ok"])
                for j in range(NH):
                    dve.wait_ge(S["conv0"], NH * c + j + 1)
                    xm = side[1 - j].rearrange("p (b t) -> p b t", b=BC)
                    acc = u[:, j, :].rearrange("p (b t) -> p b t", b=BC)
                    for s in range(1, TAPS):
                        ins = v.scalar_tensor_tensor(acc[:, :, s:T], xm[:, :, 0:T - s],
                                                     chan[:, j, TAPS - 1 - s:TAPS - s], acc[:, :, s:T], ALU.mult, ALU.add)
                        if s < TAPS - 1:
                            step(ins)
                            settle()
                    ins.then_inc(S["conv_ok"], 1)
                dve.wait_ge(S["dbc_copied"], c + 1)
                dve.wait_ge(S["dt_ok"], c + 1)
                v.scalar_tensor_tensor(dbc_t[:], dbc_hi[:], cut_g[:, 0:1], side[1][0:PARTS * G, :], ALU.mult, ALU.add
                                       ).then_inc(S["dbc_r1"], 1)
                dve.wait_ge(S["dbc_mid"], c + 1)
                v.scalar_tensor_tensor(dbc_parts[:], dbc_hi[:], cut_g[:, 1:2], dbc_t[:], ALU.mult, ALU.add
                                       ).then_inc(S["dbc_ok"], 1)
                for j in range(NH):
                    dve.wait_ge(S["dp_mm"], NH * c + j + 1)
                    v.tensor_scalar(delta[:, j, :], side[j], chan[:, j, TAPS + 1:TAPS + 2], 0.0, ALU.add, ALU.max
                                    ).then_inc(S["dp_max"], 1)

            def scan_step(k, n, buf):
                dve.wait_ge(S["drive_ok"], k + n + 1)
                if not (isinstance(n, int) and k + n < 2):
                    dve.wait_ge(S["weighted"], k + n - 1)
                for j in range(NH):
                    dve.wait_ge(S["decay_ok"], 2 * (k + n) + j + 1)
                    v.tensor_tensor_scan(state[:, buf, j * CH:(j + 1) * CH], decay[:, j, :],
                                         drive[:, buf, j * CH:(j + 1) * CH], 0.0, ALU.mult, ALU.add
                                         ).then_inc(S["scanned"], 1)

            def weight_step(k, n, buf):
                dve.wait_ge(S["c_bcast"], k + n + 1)
                dve.wait_ge(S["scanned"], 2 * (k + n) + 2)
                if not (isinstance(n, int) and k + n < 2):
                    dve.wait_ge(S["summed"], k + n - 1)
                v.tensor_tensor(part[:, buf, :].rearrange("p (h t) -> p h t", h=NH),
                                state[:, buf, :].rearrange("p (h t) -> p h t", h=NH),
                                bank_c.unsqueeze(1).to_broadcast([P, NH, CH]), ALU.mult).then_inc(S["weighted"], 1)

            def scan(c):
                k = STEPS * c
                scan_step(k, 0, 0)
                scan_step(k, 1, 1)
                weight_step(k, 0, 0)
                scan_step(k, 2, 0)
                weight_step(k, 1, 1)
                scan_step(k, 3, 1)
                weight_step(k, 2, 0)
                with dve.Fori(2, STEPS // 2) as i:
                    scan_step(k, i * 2, 0)
                    weight_step(k, i * 2 - 1, 1)
                    scan_step(k, i * 2 + 1, 1)
                    weight_step(k, i * 2, 0)
                weight_step(k, STEPS - 1, 1)

            def back(c):
                dve.wait_ge(S["summed"], STEPS * (c + 1))
                dve.wait_ge(S["z_ok"], NH * (c + 1))
                for j in range(NH):
                    ins = v.scalar_tensor_tensor(u[:, j, :], u[:, j, :], chan[:, j, TAPS + 2:TAPS + 3], ysum[:, j, :],
                                                 ALU.mult, ALU.add)
                    if j < NH - 1:
                        step(ins)
                ins.then_inc(S["y_read"], 1)
                dve.wait_ge(S["op_mm"], c + 1)
                v.tensor_tensor(h[:], side[0].rearrange("p (t d) -> p t d", d=D), h[:], ALU.add).then_inc(S["h2_ok"], 1)
                dve.wait_ge(S["h2_ok"], c + 1)
                dve.wait_ge(S["hn_tr"], c + 1)
                rms(c, S["rms2_ss"], S["rms2_rs"], S["hn2_ok"])
                dve.wait_ge(S["f2_mm"], c + 1)
                v.tensor_tensor(h[:], side[0].rearrange("p (t d) -> p t d", d=D), h[:], ALU.add).then_inc(S["f2_read"], 1)
                dve.wait_ge(S["f2_read"], c + 1)
                step(v.tensor_tensor(by_batch(h[:]), by_batch(h[:]), rows_of(c, GA), ALU.mult))
                settle()
                x1 = pay[:, chunk(c), D:2 * D]
                step(v.tensor_tensor(x1, h[:], x[:, chunk(c), :], ALU.add))
                settle()
                hm = pay[:, chunk(c), 0:D]
                norm(x1, S["ln2_var"], S["ln2_rstd"], c, hm)
                step(v.tensor_tensor(by_batch(hm), by_batch(hm), rows_of(c, CB), ALU.mult))
                settle()
                v.tensor_tensor(by_batch(hm), by_batch(hm), rows_of(c, SB), ALU.add).then_inc(S["hm_ok"], 1)
                dve.wait_ge(S["lg_mm"], c + 1)
                v.tensor_copy(logits[:, chunk(c), :], side[0][:, 0:TC * NE].rearrange("p (t e) -> p t e", e=NE)
                              ).then_inc(S["lg_ok"], 1)

            for c in range(NC):
                front(c)
                scan(c)
                back(c)

            def per_token(t):
                return t.unsqueeze(2).to_broadcast([P, NT, NE])

            dve.wait_ge(S["lg_ok"], NC)
            step(v.tensor_reduce(top[:], logits[:], AX_X, ALU.max))
            settle()
            v.tensor_tensor(sm, logits[:], per_token(top[:]), ALU.subtract).then_inc(S["e_d"], 1)
            dve.wait_ge(S["e_d"], 1)
            step(v.tensor_scalar(hot, sm, 0.0, None, ALU.is_equal))
            settle()
            step(v.tensor_tensor(hot, hot, prefer.unsqueeze(1).to_broadcast([P, NT, NE]), ALU.mult))
            settle()
            step(v.tensor_reduce(first[:], hot, AX_X, ALU.max))
            settle()
            step(v.tensor_tensor(hot, hot, per_token(first[:]), ALU.is_equal))
            settle()
            step(v.tensor_scalar(first[:], first[:], -float(CAP), float(CAP * NE), ALU.mult, ALU.add))
            dve.wait_ge(S["e_exp"], 1)
            step(v.tensor_reduce(top[:], msk, AX_X, ALU.add))
            settle()
            step(v.reciprocal(top[:], top[:]))
            settle()
            step(v.tensor_tensor(msk, hot, per_token(top[:]), ALU.mult))
            settle()
            step(v.scalar_tensor_tensor(msk, hot, -1.0, msk, ALU.add, ALU.add))
            settle()
            for k in range(PARTS):
                step(v.tensor_copy(h_parts[:, :, k, :], hot))
                step(v.tensor_copy(m_parts[:, :, k, :], msk))
                settle()
                if k < PARTS - 1:
                    step(v.tensor_tensor(msk, msk, m_parts[:, :, k, :], ALU.subtract))
                    settle()
            v.memset(junk2[:, 0, 0:1], 0.0).then_inc(S["parts_ok"], 1)
            dve.wait_ge(S["rt_tr"], 2 * NT)
            v.tensor_copy(m_rows, ps[0:PARTS * NE, 0:2, :].bitcast(BF16)).then_inc(S["hid_ok"], 1)
            for t in range(NT):
                dve.wait_ge(S["row_mm"], t + 1)
                row = ps[:, 4 * (t % 2):4 * (t % 2) + 4, :].rearrange("p b t -> p (b t)")
                mine = top[:, t:t + 1]
                if t >= 2:
                    dve.wait_ge(S["ranked"], t - 1)
                if t:
                    step(v.tensor_scalar(junk[:, t % 2, 0:t * P], row[:, 0:t * P], mine, None, ALU.is_ge, ALU.add,
                                         accum_out=cnt[:, t, 0:1]))
                else:
                    step(v.memset(cnt[:, 0, 0:1], 0.0))
                step(v.tensor_scalar(junk[:, t % 2, t * P:TOK], row[:, t * P:TOK], mine, None, ALU.is_gt, ALU.add,
                                     accum_out=cnt[:, t, 1:2]))
                v.scalar_tensor_tensor(junk2[:, t % 2, :], row[:, t * P:(t + 1) * P], mine, earlier, ALU.is_equal, ALU.mult,
                                       accum_out=cnt[:, t, 2:3]).then_inc(S["ranked"], 1)

            for s in range(0, ST, 4):
                g = s // 4
                dve.wait_ge(S["xt_tr"], g + 1)
                v.tensor_copy(xe_t[:, s * P:(s + 4) * P], ps[:, g % 2, :]).then_inc(S["xt_ok"], 1)
            done = 0
            for e in range(NE):
                dve.wait_ge(S["e2_mm"], e + 1)
                v.tensor_scalar(o_t[:, e * CAP:(e + 1) * CAP], ps[:, 4 + e % 2, 0:CAP],
                                cols[:, 2 + FB + 2 * NE + e:3 + FB + 2 * NE + e], None, ALU.add).then_inc(S["e2_ok"], 1)
                while (done + 4) * P <= (e + 1) * CAP:
                    g = done // 4
                    dve.wait_ge(S["o_tr"], g + 1)
                    f = fin[:, done:done + 4, :]
                    step(v.tensor_tensor(f, ps[:, 6 + g % 2, :].rearrange("p (s d) -> p s d", d=D),
                                         xe[:, done:done + 4, 2 * D:3 * D], ALU.mult))
                    settle()
                    v.tensor_tensor(f, f, xe[:, done:done + 4, D:2 * D], ALU.add).then_inc(S["fin_ok"], 1)
                    done += 4

        @block.tensor
        def _(pe):
            mm = nc.tensor.matmul
            pe.wait_ge(S["silu_c_ok"], 1)
            mm(side[0][0:PARTS * NB, :], silu_c[:], w_mod[:, 0:CH], start=True, stop=True).then_inc(S["mod_mm"], 1)
            mm(side[1][0:PARTS * NB, 0:6 * D - CH], silu_c[:], w_mod[:, CH:6 * D], start=True, stop=True
               ).then_inc(S["mod_mm"], 1)
            pe.wait_ge(S["mod_parts_ok"], 1)
            for b in range(NB):
                if b:
                    pe.wait_ge(S["mod_bc_copied"], 2 * b)
                    pe.wait_ge(S["gate_rows"], b)
                mm(side[0], bsel[:, b, :], mod_parts[:, 0:CH], start=True, stop=True).then_inc(S["mod_bc"], 1)
                mm(side[1][:, 0:6 * D - CH], bsel[:, b, :], mod_parts[:, CH:6 * D], start=True, stop=True
                   ).then_inc(S["mod_bc"], 1)

            def to_channels(bank, src, done):
                for t in range(TC):
                    ins = nc.tensor.transpose(bank[:, t * P:(t + 1) * P], src[:, t, :], ident)
                ins.then_inc(done, 1)

            def front(c):
                pe.wait_ge(S["hn_ok"], c + 1)
                if c:
                    pe.wait_ge(S["lg_ok"], c)
                else:
                    pe.wait_ge(S["gate_rows"], NB)
                    pe.wait_ge(S["mod_bc_copied"], 2 * NB)
                to_channels(side[0], hn, S["hn_tr"])
                pe.wait_ge(S["h_t_ok"], c + 1)
                pe.wait_ge(S["ld_w"], 16 * 5)
                for j in range(NH):
                    mm(side[1 - j], w_in[:, j * P:(j + 1) * P], h_t[:], start=True, stop=True).then_inc(S["xm_mm"], 1)
                for j in range(NH):
                    pe.wait_ge(S["conv_ok"], NH * c + j + 1)
                    mm(side[1 - j], w_in[:, DI + j * P:DI + (j + 1) * P], h_t[:], start=True, stop=True
                       ).then_inc(S["z_mm"], 1)
                pe.wait_ge(S["u_ok"], NH * (c + 1))
                pe.wait_ge(S["z_ok"], NH * c + 1)
                for j in range(NH):
                    ins = mm(side[1][0:PARTS * G, :], w_xp[:, j, :], u[:, j, :], start=(j == 0), stop=(j == NH - 1))
                ins.then_inc(S["dbc_mm"], 1)
                pe.wait_ge(S["dt_ok"], c + 1)
                pe.wait_ge(S["z_ok"], NH * (c + 1))
                pe.wait_ge(S["dbc_r1"], c + 1)
                for j in range(NH):
                    mm(side[j], w_dt[:, j * P:(j + 1) * P], dt_rows[:], start=True, stop=True).then_inc(S["dp_mm"], 1)

            def bcast_b(k, n):
                if not (isinstance(n, int) and k + n < 1):
                    pe.wait_ge(S["b_copied"], k + n)
                mm(bank_b, sel[:, bass.ds(n, 1), :].rearrange("p o c -> p (o c)"), dbc_parts[:], start=True, stop=True
                   ).then_inc(S["b_bcast"], 1)

            def bcast_c(k, n):
                if not (isinstance(n, int) and k + n < 1):
                    pe.wait_ge(S["weighted"], k + n)
                mm(bank_c, sel[:, bass.ds(n + NS, 1), :].rearrange("p o c -> p (o c)"), dbc_parts[:], start=True, stop=True
                   ).then_inc(S["c_bcast"], 1)

            def sum_step(k, n, buf, start, stop):
                pe.wait_ge(S["weighted"], k + n + 1)
                for j in range(NH):
                    ins = mm(ysum[:, j, :], ident, part[:, buf, j * CH:(j + 1) * CH], start=start, stop=stop,
                             skip_group_check=True)
                ins.then_inc(S["summed"], 1)

            def scan(c):
                k = STEPS * c
                pe.wait_ge(S["dbc_ok"], c + 1)
                if c:
                    pe.wait_ge(S["y_read"], c)
                bcast_b(k, 0)
                bcast_c(k, 0)
                bcast_b(k, 1)
                bcast_b(k, 2)
                bcast_c(k, 1)
                sum_step(k, 0, 0, True, False)
                with pe.Fori(0, STEPS // 2 - 2) as i:
                    for s in (1, 2):
                        bcast_b(k, i * 2 + s + 2)
                        bcast_c(k, i * 2 + s + 1)
                        sum_step(k, i * 2 + s, s % 2, False, False)
                bcast_b(k, STEPS - 1)
                for n in (STEPS - 3, STEPS - 2):
                    bcast_c(k, n + 1)
                    sum_step(k, n, n % 2, False, False)
                sum_step(k, STEPS - 1, 1, False, True)

            def back(c):
                pe.wait_ge(S["ld_m"], 16 * 5)
                pe.wait_ge(S["yg_ok"], c + 1)
                pe.wait_ge(S["dp_abs"], NH * (c + 1))
                for t in range(TC):
                    for j in range(NH):
                        ins = mm(side[0][:, t * D:(t + 1) * D], u[:, j, t * P:(t + 1) * P], w_out[:, j, :],
                                 start=(j == 0), stop=(j == NH - 1))
                ins.then_inc(S["op_mm"], 1)
                pe.wait_ge(S["hn2_ok"], c + 1)
                to_channels(side[1], hn, S["hn2_tr"])
                pe.wait_ge(S["h2_t_ok"], c + 1)
                for f in range(FB):
                    if f >= 2:
                        pe.wait_ge(S["gelu_ok"], FB * c + f - 1)
                    mm(side[f % 2], w_m1[:, f * P:(f + 1) * P], h_t[:], start=True, stop=True).then_inc(S["f1_mm"], 1)
                pe.wait_ge(S["sel_ok"], 1)
                pe.wait_ge(S["gelu_ok"], FB * (c + 1))
                for t in range(TC):
                    mm(side[0][:, t * D:(t + 1) * D], ones[:], b2row[:], start=True, stop=False)
                    for f in range(FB):
                        ins = mm(side[0][:, t * D:(t + 1) * D], m_t[:, f, t * P:(t + 1) * P], w_m2[:, f, :],
                                 start=False, stop=(f == FB - 1))
                ins.then_inc(S["f2_mm"], 1)
                pe.wait_ge(S["hm_ok"], c + 1)
                to_channels(side[1], pay[:, chunk(c), 0:D], S["hm_tr"])
                pe.wait_ge(S["hm_t_ok"], c + 1)
                for t in range(TC):
                    ins = mm(side[0][:, t * NE:(t + 1) * NE], h_t[:, t * P:(t + 1) * P], w_g[:], start=True, stop=True)
                ins.then_inc(S["lg_mm"], 1)

            for c in range(NC):
                front(c)
                scan(c)
                back(c)

            pe.wait_ge(S["parts_ok"], 1)
            ps16 = ps[:, 0:4, :].bitcast(BF16)
            for k, src in enumerate((m_parts, h_parts)):
                for t in range(NT):
                    half_bank = ps16[0:PARTS * NE, 2 * k + t // 8, (t % 8) * P:(t % 8 + 1) * P]
                    nc.tensor.transpose(half_bank, src[:, t, :, :].rearrange("p k e -> p (k e)"), id16[:]
                                        ).then_inc(S["rt_tr"], 1)
            pe.wait_ge(S["rt_rows"], 1)
            pe.wait_ge(S["hid_ok"], 1)
            for t in range(NT):
                if t >= 2:
                    pe.wait_ge(S["ranked"], t - 1)
                for b in range(4):
                    ins = mm(ps[:, 4 * (t % 2) + b, :], h_rows[:, t * P:(t + 1) * P], m_rows[:, b * CH:(b + 1) * CH],
                             start=True, stop=True)
                ins.then_inc(S["row_mm"], 1)

            pe.wait_ge(S["ld_e"], 32)
            pe.wait_ge(S["ranked"], NT)
            pe.wait_ge(S["xe_in"], 16 * (ST // 4))
            for g in range(ST // 4):
                if g >= 2:
                    pe.wait_ge(S["xt_ok"], g - 1)
                for s in range(4):
                    ins = nc.tensor.transpose(ps[:, g % 2, s * P:(s + 1) * P], xe[:, 4 * g + s, 0:D], ident)
                ins.then_inc(S["xt_tr"], 1)

            def up(e):
                pe.wait_ge(S["xt_ok"], -(-(e + 1) * CAP // CH))
                if e >= 2:
                    pe.wait_ge(S["e1_ok"], 2 * (e - 1))
                for j in range(2):
                    ins = mm(ps[:, 2 + e % 2, j * CAP:(j + 1) * CAP], w_e1[:, e, j * P:(j + 1) * P],
                             xe_t[:, e * CAP:(e + 1) * CAP], start=True, stop=True)
                ins.then_inc(S["e1_mm"], 1)

            def down(e):
                pe.wait_ge(S["e1_ok"], 2 * (e + 1))
                if e >= 2:
                    pe.wait_ge(S["e2_ok"], e - 1)
                for j in range(2):
                    ins = mm(ps[:, 4 + e % 2, 0:CAP], w_e2[:, e, j, :], g_t[:, e % 2, j, :], start=(j == 0), stop=(j == 1))
                ins.then_inc(S["e2_mm"], 1)

            def to_slots(g):
                pe.wait_ge(S["e2_ok"], -(-(g + 1) * CH // CAP))
                if g >= 2:
                    pe.wait_ge(S["fin_ok"], g - 1)
                for s in range(4):
                    ins = nc.tensor.transpose(ps[:, 6 + g % 2, s * P:(s + 1) * P],
                                              o_t[:, (4 * g + s) * P:(4 * g + s + 1) * P], ident)
                ins.then_inc(S["o_tr"], 1)

            up(0)
            g = 0
            for e in range(NE):
                if e + 1 < NE:
                    up(e + 1)
                down(e)
                while (g + 1) * CH <= e * CAP:
                    to_slots(g)
                    g += 1
            while g < SLOTS // CH:
                to_slots(g)
                g += 1


def kernel(**inputs):
    import numpy as np
    import concourse.bacc as bacc
    from concourse.bass_utils import run_bass_kernel_spmd as run

    def arr(n):
        return np.asarray(inputs["L0_" + n])

    def lay(v):
        return np.ascontiguousarray(v)

    def by_part(v, parts):
        return lay(v.reshape(parts, P, -1).transpose(1, 0, 2))

    f = np.float32
    consts = np.zeros((P, 3 * P + 2 * NS + 64), f)
    consts[:, 0:P] = np.eye(P)
    consts[:, P:2 * P] = np.tril(np.ones((P, P)), -1)
    consts[:, 2 * P:2 * P + NT] = np.arange(P)[:, None] + P * np.arange(NT)[None, :] + 1
    consts[:, 2 * P + NT:2 * P + NT + NE] = NE - np.arange(NE)[None, :]
    o = 2 * P + NT + NE
    for k in range(PARTS):
        for n in range(2 * NS):
            consts[k * G + RANK + n, o + n] = 1
        for b in range(NB):
            consts[k * NB + b, o + 2 * NS + b] = 1
    o += 2 * NS + NB
    consts[G:PARTS * G, o] = -1
    consts[2 * G:PARTS * G, o + 1] = -1
    consts[NB:PARTS * NB, o + 2] = -1
    consts[2 * NB:PARTS * NB, o + 3] = -1
    consts[:, o + 4:o + 4 + TC] = -0.5

    x_proj = arr("attn_x_proj_w").T
    chan = np.concatenate([arr("attn_conv_w")[:, 0, :], arr("attn_conv_b")[:, None], arr("attn_dt_proj_b")[:, None],
                           arr("attn_D")[:, None], arr("attn_A_log")], 1)
    cols = np.concatenate([arr("attn_norm1_w")[:, None], arr("attn_norm2_w")[:, None],
                           arr("attn_mlp_b1").reshape(FB, P).T, arr("ffn_b1").reshape(NE * 2, P).T,
                           arr("ffn_b2").T], 1)
    arrays = {
        "x": lay(arr("attn_x").reshape(NT, P, D).transpose(1, 0, 2)),
        "c_t": lay(np.concatenate([arr("c").T] * PARTS, 1)),
        "w_mod": lay(arr("wmod")),
        "consts": consts,
        "cols": lay(cols),
        "chan": by_part(chan, NH),
        "w_in": lay(arr("attn_in_proj_w").T),
        "w_xp": by_part(np.concatenate([x_proj] * PARTS, 1), NH),
        "w_dt": lay(arr("attn_dt_proj_w").T),
        "w_out": by_part(arr("attn_out_proj_w").T, NH),
        "w_m1": lay(arr("attn_mlp_w1").T),
        "w_m2": by_part(arr("attn_mlp_w2").T, FB),
        "b2row": lay(arr("attn_mlp_b2")[None, :]),
        "w_g": lay(arr("ffn_Wg")),
        "w_e1": lay(arr("ffn_W1").transpose(1, 0, 2)),
        "w_e2": lay(arr("ffn_W2").reshape(NE, H // P, P, D).transpose(2, 0, 1, 3)),
    }
    nc = bacc.Bacc("TRN2", target_bir_lowering=False, num_devices=1)
    a = {n: nc.dram_tensor("in_" + n, v.shape, F32, kind="ExternalInput").ap() for n, v in arrays.items()}
    out = nc.dram_tensor("out_0", (NB, T, D), F32, kind="ExternalOutput").ap()
    xe_dram = nc.dram_tensor("xe_rows", (SLOTS, W_PAY), F32, kind="Internal").ap()
    adaln_mamba_moe(nc, a, out, xe_dram, None)
    r = run(nc, [{"in_" + n: v for n, v in arrays.items()}], core_ids=[0])
    return r.results[0]["out_0"]
```

```python
from contextlib import ExitStack

import concourse.bass as bass
from concourse import mybir

F32 = mybir.dt.float32
BF16 = mybir.dt.bfloat16
U32 = mybir.dt.uint32
ALU = mybir.AluOpType
ACT = mybir.ActivationFunctionType
AX_X = mybir.AxisListType.X

P = 128
NB, T = 8, 256
D = 128
DI = 2 * D
NH = DI // P
NS = 16
RANK = D // 16
TAPS = 4
F = 4 * D
FB = F // P
TOK = NB * T
NT = TOK // P
CH = 512
NC = TOK // CH
TC = CH // P
BC = CH // T
NE, H = 16, 256
CAP = -(-5 * TOK // (4 * NE))
SLOTS = NE * CAP
ST = SLOTS // P
G = RANK + 2 * NS
PARTS = 3
W_PAY = 3 * D + 1
SA, CA, GA, SB, CB, GB = range(6)
FAR = 8192.0
STEPS = NS


LN_V, LN_P, LNA_V, RMS_P, RMSA_V, TR_T, HT_A, XM_T, TAP_A, TAP0_V, TAP1_V = 0, 2, 2, 5, 4, 4, 6, 6, 8, 7, 8
Z_T, SILU_A, XP_T, PART1_A, REST_V, PART2_A, PARTS_V, DT_T, POS_V, SOFT_A = 8, 10, 10, 12, 11, 13, 12, 13, 14, 15
GATE_P, OP_T, RES_V, RMS2_P, RMS2A_V, TR2_T, H2T_A, UP_T, GELU_A = 1, 1, 2, 5, 4, 5, 7, 11, 14
DOWN_T, STREAM_V, LN2_P, LN2A_V, STAY_P, TR3_T, HMT_A, LG_T, LG_V = 0, 1, 4, 3, 8, 3, 5, 4, 5


def BESIDE(stages):
    def at(c, n):
        for step, stage, lag in stages:
            if step == n and 0 <= c + lag < NC:
                stage(c + lag)
    return at


def adaln_mamba_moe(nc, a, out, xe_dram, dbg):
    with ExitStack() as ctx:
        def sb(name, shape, dt=F32):
            return ctx.enter_context(nc.sbuf_tensor(name, shape, dt))

        def sem(name):
            return ctx.enter_context(nc.semaphore(name))

        x = sb("x", [P, NT, D])
        w_in = sb("w_in", [D, 2 * DI])
        w_xp = sb("w_xp", [P, NH, PARTS * G])
        w_dt = sb("w_dt", [RANK, DI])
        w_out = sb("w_out", [P, NH, D])
        w_m1 = sb("w_m1", [D, F])
        w_m2 = sb("w_m2", [P, FB, D])
        w_g = sb("w_g", [D, NE])
        chan = sb("chan", [P, NH, TAPS + 3 + NS])
        cols = sb("cols", [P, 2 + FB + 2 * NE + NE])
        b2row = sb("b2row", [1, D])
        c_t = sb("c_t", [D, PARTS * NB])
        w_mod = sb("w_mod", [D, 6 * D])
        consts = sb("consts", [P, 3 * P + 2 * NS + 64])
        ident = consts[:, 0:P]
        earlier = consts[:, P:2 * P]
        token1 = consts[:, 2 * P:2 * P + NT]
        prefer = consts[:, 2 * P + NT:2 * P + NT + NE]
        o_ = 2 * P + NT + NE
        sel_rows = consts[0:PARTS * G, o_:o_ + 2 * NS]
        o_ += 2 * NS
        sel_batch = consts[0:PARTS * NB, o_:o_ + NB]
        o_ += NB
        cut_g = consts[0:PARTS * G, o_:o_ + 2]
        cut_m = consts[0:PARTS * NB, o_ + 2:o_ + 4]
        half = consts[:, o_ + 4:o_ + 4 + TC]
        ones = sb("ones", [1, P])
        id16 = sb("id16", [P, P], BF16)
        sel = sb("sel", [PARTS * G, 2 * NS, P], BF16)
        bsel = sb("bsel", [PARTS * NB, NB, P], BF16)
        neg_a = sb("neg_a", [P, NH, NS])

        silu_c = sb("silu_c", [D, PARTS * NB])
        mod_b = sb("mod_b", [P, NB, 5 * D])

        bn = sb("bn", [P, 2, TC, 6])
        mv = sb("mv", [P, 2, TC, 2])
        ss = sb("ss", [P, 2, TC])
        rs = sb("rs", [P, 4, TC])

        h = sb("h", [P, 4, TC, D])
        hn = sb("hn", [P, 2, TC, D])
        h_t = sb("h_t", [D, 2, CH])
        pay = sb("pay", [P, NT, W_PAY])
        base = sb("base", [P, TC, D])
        logits = sb("logits", [P, NT, NE])

        ARENA = 24576
        arena = sb("arena", [P, ARENA])
        at = [0]

        def take(n):
            at[0] += n
            assert at[0] <= ARENA, at[0]
            return arena[:, at[0] - n:at[0]]

        def halves(k):
            return take(k * NH * CH).rearrange("p (k h t) -> p k h t", k=k, h=NH)

        u, zg, delta, du = halves(2), halves(2), halves(2), halves(2)
        soft = take(NH * CH).rearrange("p (h t) -> p h t", h=NH)
        b_rows = take(4 * CH).rearrange("p (k t) -> p k t", k=4)
        drive = take(2 * NH * CH).rearrange("p (k t) -> p k t", k=2)
        state = take(4 * NH * CH).rearrange("p (k t) -> p k t", k=4)
        part = take(2 * NH * CH).rearrange("p (k t) -> p k t", k=2)
        m_t = take(FB * CH).rearrange("p (f t) -> p f t", f=FB)
        m_ = state.rearrange("p k t -> p (k t)")[0:PARTS * NB, :]
        mod, mod_t = m_[:, 0:6 * D], m_[:, 6 * D:12 * D]
        mod_hi = m_[:, 12 * D:15 * D].bitcast(BF16)
        mod_parts = m_[:, 15 * D:18 * D].bitcast(BF16)
        at[0] = 0
        xe = take(ST * W_PAY).rearrange("p (s w) -> p s w", w=W_PAY)
        xe_t = take(SLOTS)
        o_t = take(SLOTS)
        fin = take(SLOTS).rearrange("p (s d) -> p s d", d=D)
        g_t = take(2 * 2 * CAP).rearrange("p (k h s) -> p k h s", k=2, h=2)
        w_e1 = take(NE * H).rearrange("p (e h) -> p e h", e=NE)
        w_e2 = take(NE * H).rearrange("p (e k d) -> p e k d", e=NE, k=H // P)
        dbc_hi = sb("dbc_hi", [PARTS * G, CH], BF16)
        dbc_t = sb("dbc_t", [PARTS * G, CH])
        dbc_parts = sb("dbc_parts", [PARTS * G, 2, CH], BF16)
        dt_rows = sb("dt_rows", [RANK, CH])

        at[0] = 0
        sm = take(NT * NE).rearrange("p (t e) -> p t e", e=NE)
        hot = take(NT * NE).rearrange("p (t e) -> p t e", e=NE)
        msk = take(NT * NE).rearrange("p (t e) -> p t e", e=NE)
        msk_r = take(NT * NE).rearrange("p (t e) -> p t e", e=NE)
        m_parts = take(NT * PARTS * NE // 2).bitcast(BF16).rearrange("p (t k e) -> p t k e", k=PARTS, e=NE)
        h_parts = take(NT * PARTS * NE // 2).bitcast(BF16).rearrange("p (t k e) -> p t k e", k=PARTS, e=NE)
        m_rows = take(TOK // 2)[0:PARTS * NE, :].bitcast(BF16)
        h_rows = take(TOK // 2)[0:PARTS * NE, :].bitcast(BF16)
        junk = take(TOK).bitcast(BF16).rearrange("p (k t) -> p k t", k=2)
        junk2 = take(2 * P).rearrange("p (k t) -> p k t", k=2)
        top = sb("top", [P, NT])
        first = sb("first", [P, NT])
        cnt = sb("cnt", [P, NT, 3])
        slot_f = sb("slot_f", [P, NT, 4])
        slot = sb("slot", [P, NT], U32)
        tok_f = sb("tok_f", [P, ST, 2])
        tok = sb("tok", [P, ST], U32)
        zeros = m_t.rearrange("p f t -> p (f t)")[:, 0:4 * W_PAY]

        ps = ctx.enter_context(nc.psum_tensor("ps", [P, 8, CH], F32))
        bank_b, bank_c = ps[:, 0, :], ps[:, 1, :]
        decay = ps[:, 2:4, :]
        ysum = ps[:, 4:6, :]
        side = [ps[:, 6, :], ps[:, 7, :]]

        block = ctx.enter_context(nc.Block())
        S = {n: sem(n) for n in (
            "ld_mod", "ld_const", "ld_w", "ld_m", "ld_e", "dram_zeroed", "base_out", "rows_out", "xe_in", "rg_in", "final_out",
            "silu_c_ok", "mod_mm", "mod_raw", "mod_hi_ok", "mod_parts_ok", "mod_bc", "mod_bc_copied", "mod_bc_copied_v",
            "gate_rows", "sel_ok", "decay_zeroed", "neg_a_ok",
            "ln_var", "ln_rstd", "rms_ss", "rms_rs", "hn_ok", "hn_tr", "h_t_ok",
            "xm_mm", "conv0", "conv_ok", "u_ok", "z_mm", "z_ok", "dbc_mm", "dbc_copied", "dbc_r1", "dbc_mid", "dbc_ok",
            "dt_ok", "dp_mm", "dp_abs", "dp_max", "dp_ln", "delta_ok", "du_ok",
            "b_bcast", "b_copied", "drive_ok", "decay_ok", "scanned", "c_bcast", "weighted", "summed",
            "y_read", "yg_ok", "op_mm", "h2_ok", "rms2_ss", "rms2_rs", "hn2_ok", "hn2_tr", "h2_t_ok", "f1_mm", "gelu_ok",
            "f2_mm", "f2_read", "x1_stats", "ln2_var", "ln2_rstd", "hm_ok", "hm_tr", "hm_t_ok", "lg_mm", "lg_ok", "base_ok", "x1_ok",
            "e_exp", "e_d", "parts_ok", "hid_ok", "rt_tr", "rt_rows", "row_mm", "ranked", "slot_ok", "zero_ok",
            "xt_tr", "xt_ok", "e1_mm", "e1_ok", "e2_mm", "e2_ok", "o_tr", "fin_ok", "tok_ok",
            "dve_step", "act_step", "pool_step")}
        S["ld_x"] = [sem(f"ld_x{c}") for c in range(NC)]

        def chunk(c):
            return slice(TC * c, TC * (c + 1))

        @block.sync
        def _(sp):
            sp.dma_start(c_t[:], a["c_t"]).then_inc(S["ld_mod"], 16)
            sp.dma_start(w_mod[:], a["w_mod"]).then_inc(S["ld_mod"], 16)
            sp.dma_start(consts[:], a["consts"]).then_inc(S["ld_const"], 16)
            for c in range(NC):
                sp.dma_start(x[:, chunk(c), :], a["x"][:, chunk(c), :]).then_inc(S["ld_x"][c], 16)
                if c == 0:
                    sp.dma_start(cols[:], a["cols"]).then_inc(S["ld_w"], 16)
                    sp.dma_start(chan[:], a["chan"]).then_inc(S["ld_w"], 16)
                    sp.dma_start(w_in[:], a["w_in"]).then_inc(S["ld_w"], 16)
                    sp.dma_start(w_xp[:], a["w_xp"]).then_inc(S["ld_w"], 16)
                    sp.dma_start(w_dt[:], a["w_dt"]).then_inc(S["ld_w"], 16)
            sp.dma_start(w_out[:], a["w_out"]).then_inc(S["ld_m"], 16)
            sp.dma_start(w_m1[:], a["w_m1"]).then_inc(S["ld_m"], 16)
            sp.dma_start(w_m2[:], a["w_m2"]).then_inc(S["ld_m"], 16)
            sp.dma_start(b2row[:], a["b2row"]).then_inc(S["ld_m"], 16)
            sp.dma_start(w_g[:], a["w_g"]).then_inc(S["ld_m"], 16)
            sp.wait_ge(S["zero_ok"], 1)
            rows = xe_dram.rearrange("(p s) w -> p (s w)", p=P)
            for s in range(0, ST, 4):
                sp.dma_start(rows[:, s * W_PAY:(s + 4) * W_PAY], zeros).then_inc(S["dram_zeroed"], 16)
            ov = out.rearrange("b (t p) d -> p (b t) d", p=P)
            for c in range(NC):
                sp.wait_ge(S["base_ok"], c + 1)
                sp.dma_start(ov[:, chunk(c), :], base[:]).then_inc(S["base_out"], 16)
            sp.dma_start(w_e1, a["w_e1"]).then_inc(S["ld_e"], 16)
            sp.dma_start(w_e2, a["w_e2"]).then_inc(S["ld_e"], 16)
            sp.wait_ge(S["rows_out"], 16 * NT)
            xv = xe_dram.rearrange("(s p) w -> p s w", p=P)
            for s in range(0, ST, 4):
                sp.dma_start(xe[:, s:s + 4, :], xv[:, s:s + 4, :]).then_inc(S["xe_in"], 16)
            sp.wait_ge(S["base_out"], 16 * NC)
            sp.wait_ge(S["final_out"], 16 * ST)

        @block.gpsimd
        def _(gp):
            n_step = [0]

            def step(ins):
                n_step[0] += 1
                ins.then_inc(S["pool_step"], 1)

            def settle():
                gp.wait_ge(S["pool_step"], n_step[0])

            nc.gpsimd.memset(zeros, 0.0).then_inc(S["zero_ok"], 1)
            nc.gpsimd.memset(ones[:], 1.0).then_inc(S["sel_ok"], 1)
            gp.wait_ge(S["ld_const"], 16)
            step(nc.gpsimd.tensor_copy(pay[:, :, 3 * D], token1))

            def inverse_root(which, src, eps, ready, done, k):
                gp.wait_ge(ready, k + 1)
                step(nc.gpsimd.tensor_scalar(rs[:, which, :], src, eps, None, ALU.add))
                settle()
                nc.gpsimd.tensor_tensor(rs[:, which, :], rs[:, which, :], half, ALU.pow).then_inc(done, 1)

            def ln_rstd(k):
                inverse_root(0, mv[:, 0, :, 1], 1e-5, S["ln_var"], S["ln_rstd"], k)

            def rms_rs(k):
                inverse_root(1, ss[:, 0, :], 1e-6, S["rms_ss"], S["rms_rs"], k)

            def rms2_rs(k):
                inverse_root(2, ss[:, 1, :], 1e-6, S["rms2_ss"], S["rms2_rs"], k)

            def ln2_rstd(k):
                inverse_root(3, mv[:, 1, :, 1], 1e-5, S["ln2_var"], S["ln2_rstd"], k)

            def step_sizes(k):
                b = k % 2
                gp.wait_ge(S["dp_ln"], NH * (k + 1))
                gp.wait_ge(S["dp_max"], NH * (k + 1))
                gp.wait_ge(S["u_ok"], NH * (k + 1))
                nc.gpsimd.tensor_tensor(delta[:, b], delta[:, b], soft, ALU.add).then_inc(S["delta_ok"], 1)
                gp.wait_ge(S["delta_ok"], k + 1)
                nc.gpsimd.tensor_tensor(du[:, b], delta[:, b], u[:, b], ALU.mult).then_inc(S["du_ok"], 1)

            def gate_y(k):
                gp.wait_ge(S["y_read"], k + 1)
                nc.gpsimd.tensor_tensor(u[:, k % 2], u[:, k % 2], zg[:, k % 2], ALU.mult).then_inc(S["yg_ok"], 1)

            def stay(k):
                gp.wait_ge(S["hm_ok"], k + 1)
                gp.wait_ge(S["gate_rows"], NB)
                if k:
                    gp.wait_ge(S["base_out"], 16 * k)
                t = pay[:, chunk(k), :]
                step(nc.gpsimd.tensor_tensor(base[:], t[:, :, 0:D], t[:, :, 2 * D:3 * D], ALU.mult))
                settle()
                nc.gpsimd.tensor_tensor(base[:], base[:], t[:, :, D:2 * D], ALU.add).then_inc(S["base_ok"], 1)

            def drive_step(c, n):
                k = STEPS * c + n
                gp.wait_ge(S["b_copied"], k + 1)
                if k >= 2:
                    gp.wait_ge(S["scanned"], NH * (k - 1))
                nc.gpsimd.tensor_tensor(
                    drive[:, n % 2, :].rearrange("p (h t) -> p h t", h=NH), du[:, c % 2],
                    b_rows[:, n % 4, :].unsqueeze(1).to_broadcast([P, NH, CH]), ALU.mult).then_inc(S["drive_ok"], 1)

            beside = BESIDE(((LN_P, ln_rstd, 1), (RMS_P, rms_rs, 1), (GATE_P, gate_y, -1), (RMS2_P, rms2_rs, -1),
                             (LN2_P, ln2_rstd, -2), (STAY_P, stay, -2)))
            ln_rstd(0)
            rms_rs(0)
            step_sizes(0)
            for c in range(NC):
                gp.wait_ge(S["du_ok"], c + 1)
                for n in range(STEPS):
                    drive_step(c, n)
                    beside(c, n)
                if c + 1 < NC:
                    step_sizes(c + 1)
            gate_y(NC - 1)
            ln2_rstd(NC - 2)
            rms2_rs(NC - 1)
            stay(NC - 2)
            ln2_rstd(NC - 1)
            stay(NC - 1)

            gp.wait_ge(S["dram_zeroed"], 16 * (ST // 4))
            for t in range(NT):
                gp.wait_ge(S["ranked"], t + 1)
                s = slot_f[:, t, :]
                step(nc.gpsimd.tensor_tensor(s[:, 0:1], cnt[:, t, 0:1], cnt[:, t, 1:2], ALU.add))
                settle()
                step(nc.gpsimd.tensor_tensor(s[:, 1:2], s[:, 0:1], cnt[:, t, 2:3], ALU.add))
                settle()
                step(nc.gpsimd.tensor_scalar(s[:, 2:3], s[:, 1:2], float(CAP), FAR, ALU.is_ge, ALU.mult))
                step(nc.gpsimd.tensor_tensor(s[:, 3:4], s[:, 1:2], first[:, t:t + 1], ALU.add))
                settle()
                nc.gpsimd.tensor_tensor(slot_f[:, t, 0:1], s[:, 2:3], s[:, 3:4], ALU.add).then_inc(S["slot_ok"], 1)
                gp.wait_ge(S["slot_ok"], 2 * t + 1)
                nc.gpsimd.tensor_copy(slot[:, t:t + 1], slot_f[:, t, 0:1]).then_inc(S["slot_ok"], 1)
                gp.wait_ge(S["slot_ok"], 2 * t + 2)
                nc.gpsimd.indirect_dma_start(
                    xe_dram, bass.IndirectOffsetOnAxis(ap=slot[:, t:t + 1], axis=0), pay[:, t, :], None,
                    bounds_check=SLOTS - 1, oob_is_err=False).then_inc(S["rows_out"], 16)

            gp.wait_ge(S["xe_in"], 16 * (ST // 4))
            step(nc.gpsimd.tensor_scalar(tok_f[:, :, 0], xe[:, :, 3 * D], 0.0, FAR, ALU.is_equal, ALU.mult))
            step(nc.gpsimd.tensor_scalar(tok_f[:, :, 1], xe[:, :, 3 * D], -1.0, None, ALU.add))
            settle()
            step(nc.gpsimd.tensor_tensor(tok_f[:, :, 0], tok_f[:, :, 0], tok_f[:, :, 1], ALU.add))
            settle()
            step(nc.gpsimd.tensor_copy(tok[:], tok_f[:, :, 0]))
            settle()
            gp.wait_ge(S["base_out"], 16 * NC)
            flat = out.rearrange("b t d -> (b t) d")
            for s in range(ST):
                gp.wait_ge(S["fin_ok"], s // 4 + 1)
                nc.gpsimd.indirect_dma_start(
                    flat, bass.IndirectOffsetOnAxis(ap=tok[:, s:s + 1], axis=0), fin[:, s, :], None,
                    bounds_check=TOK - 1, oob_is_err=False).then_inc(S["final_out"], 16)

        @block.scalar
        def _(act):
            act.wait_ge(S["ld_mod"], 32)
            nc.scalar.activation(silu_c[:], c_t[:], ACT.Silu).then_inc(S["silu_c_ok"], 1)
            act.wait_ge(S["mod_mm"], 2)
            nc.scalar.activation(mod[:, 0:CH], side[0][0:PARTS * NB, :], ACT.Copy).then_inc(S["mod_raw"], 1)
            nc.scalar.activation(mod[:, CH:6 * D], side[1][0:PARTS * NB, 0:6 * D - CH], ACT.Copy).then_inc(S["mod_raw"], 1)
            act.wait_ge(S["ld_w"], 16 * 5)
            nc.scalar.activation(neg_a[:], chan[:, :, TAPS + 3:], ACT.Exp).then_inc(S["act_step"], 1)
            for b in range(0, NB, 1):
                act.wait_ge(S["mod_bc"], 2 * b + 2)
                nc.scalar.activation(mod_b[:, b, 0:CH], side[0], ACT.Copy).then_inc(S["mod_bc_copied"], 1)
                nc.scalar.activation(mod_b[:, b, CH:5 * D], side[1][:, 0:D], ACT.Copy).then_inc(S["mod_bc_copied"], 1)

            def to_h_t(k):
                act.wait_ge(S["hn_tr"], k + 1)
                if k:
                    act.wait_ge(S["z_mm"], NH * k)
                nc.scalar.activation(h_t[:, 0, :], side[0], ACT.Copy, scale=cols[:, 0:1]).then_inc(S["h_t_ok"], 1)

            def last_tap(k):
                if k >= 2:
                    act.wait_ge(S["op_mm"], k - 1)
                for j in range(NH):
                    act.wait_ge(S["xm_mm"], NH * k + j + 1)
                    nc.scalar.activation(u[:, k % 2, j, :], side[j], ACT.Identity, bias=chan[:, j, TAPS:TAPS + 1],
                                         scale=chan[:, j, TAPS - 1:TAPS]).then_inc(S["conv0"], 1)

            def silus(k):
                for j in range(NH):
                    act.wait_ge(S["conv_ok"], NH * k + j + 1)
                    nc.scalar.activation(u[:, k % 2, j, :], u[:, k % 2, j, :], ACT.Silu).then_inc(S["u_ok"], 1)
                if k >= 2:
                    act.wait_ge(S["yg_ok"], k - 1)
                for j in range(NH):
                    act.wait_ge(S["z_mm"], NH * k + j + 1)
                    nc.scalar.activation(zg[:, k % 2, j, :], side[j], ACT.Silu).then_inc(S["z_ok"], 1)

            def first_part(k):
                act.wait_ge(S["dbc_mm"], k + 1)
                if k:
                    act.wait_ge(S["dbc_ok"], k)
                    act.wait_ge(S["dp_mm"], NH * k)
                nc.scalar.activation(dbc_hi[:], side[0][0:PARTS * G, :], ACT.Copy).then_inc(S["dbc_copied"], 1)
                nc.scalar.activation(dt_rows[:], side[0][0:RANK, :], ACT.Copy).then_inc(S["dt_ok"], 1)

            def second_part(k):
                act.wait_ge(S["dbc_r1"], k + 1)
                nc.scalar.activation(dbc_hi[:], dbc_t[:], ACT.Copy).then_inc(S["dbc_mid"], 1)

            def softplus(k):
                if k:
                    act.wait_ge(S["delta_ok"], k)
                for j in range(NH):
                    act.wait_ge(S["dp_max"], NH * k + j + 1)
                    nc.scalar.activation(soft[:, j, :], side[j], ACT.Abs, bias=chan[:, j, TAPS + 1:TAPS + 2]
                                         ).then_inc(S["dp_abs"], 1)
                act.wait_ge(S["dp_abs"], NH * (k + 1))
                nc.scalar.activation(soft, soft, ACT.Exp, scale=-1.0).then_inc(S["act_step"], 1)
                act.wait_ge(S["act_step"], k + 2)
                nc.scalar.activation(soft, soft, ACT.Ln, bias=1.0).then_inc(S["dp_ln"], NH)

            def to_h2_t(k):
                act.wait_ge(S["hn2_tr"], k + 1)
                if k:
                    act.wait_ge(S["lg_mm"], k)
                nc.scalar.activation(h_t[:, 1, :], side[1], ACT.Copy, scale=cols[:, 1:2]).then_inc(S["h2_t_ok"], 1)

            def gelus(k):
                if k == 0:
                    act.wait_ge(S["dram_zeroed"], 16 * (ST // 4))
                else:
                    act.wait_ge(S["f2_mm"], k)
                for f in range(FB):
                    act.wait_ge(S["f1_mm"], FB * k + f + 1)
                    nc.scalar.activation(m_t[:, f, :], side[1 - f % 2], ACT.Gelu, bias=cols[:, 2 + f:3 + f]
                                         ).then_inc(S["gelu_ok"], 1)

            def to_hm_t(k):
                act.wait_ge(S["hm_tr"], k + 1)
                act.wait_ge(S["f1_mm"], FB * (k + 1))
                nc.scalar.activation(h_t[:, 1, :], side[1], ACT.Copy).then_inc(S["hm_t_ok"], 1)

            def copy_b(c, n):
                k = STEPS * c + n
                act.wait_ge(S["b_bcast"], k + 1)
                if k >= 4:
                    act.wait_ge(S["drive_ok"], k - 3)
                nc.scalar.activation(b_rows[:, n % 4, :], bank_b, ACT.Copy).then_inc(S["b_copied"], 1)

            def decay_step(c, n):
                k = STEPS * c + n
                for j in range(NH):
                    if k:
                        act.wait_ge(S["scanned"], NH * (k - 1) + j + 1)
                    nc.scalar.activation(decay[:, j, :].rearrange("p (b t) -> p b t", b=BC)[:, :, 1:T],
                                         delta[:, c % 2, j, :].rearrange("p (b t) -> p b t", b=BC)[:, :, 1:T], ACT.Exp,
                                         scale=neg_a[:, j, n:n + 1]).then_inc(S["decay_ok"], 1)

            beside = BESIDE(((HT_A, to_h_t, 1), (TAP_A, last_tap, 1), (SILU_A, silus, 1), (PART1_A, first_part, 1),
                             (PART2_A, second_part, 1), (SOFT_A, softplus, 1),
                             (H2T_A, to_h2_t, -1), (GELU_A, gelus, -1), (HMT_A, to_hm_t, -2)))
            to_h_t(0)
            last_tap(0)
            silus(0)
            first_part(0)
            second_part(0)
            softplus(0)
            act.wait_ge(S["neg_a_ok"], 1)
            act.wait_ge(S["decay_zeroed"], 1)
            for c in range(NC):
                for n in range(3):
                    copy_b(c, n)
                act.wait_ge(S["delta_ok"], c + 1)
                for n in range(STEPS):
                    decay_step(c, n)
                    beside(c, n)
                    if n + 3 < STEPS:
                        copy_b(c, n + 3)
            to_hm_t(NC - 2)
            to_h2_t(NC - 1)
            gelus(NC - 1)
            to_hm_t(NC - 1)

            act.wait_ge(S["e_d"], 1)
            nc.scalar.activation(msk, sm, ACT.Exp).then_inc(S["e_exp"], 1)
            act.wait_ge(S["rt_tr"], 2 * NT)
            nc.scalar.activation(h_rows, ps[0:PARTS * NE, 2:4, :].bitcast(BF16), ACT.Copy).then_inc(S["rt_rows"], 1)
            for e in range(NE):
                act.wait_ge(S["e1_mm"], e + 1)
                if e >= 2:
                    act.wait_ge(S["e2_mm"], e - 1)
                for j in range(2):
                    nc.scalar.activation(g_t[:, e % 2, j, :], ps[:, 2 + e % 2, j * CAP:(j + 1) * CAP], ACT.Gelu_apprx_tanh,
                                         bias=cols[:, 2 + FB + 2 * e + j:3 + FB + 2 * e + j]).then_inc(S["e1_ok"], 1)

        @block.vector
        def _(dve):
            n_step = [0]

            def step(ins):
                n_step[0] += 1
                ins.then_inc(S["dve_step"], 1)

            def settle():
                dve.wait_ge(S["dve_step"], n_step[0])

            v = nc.vector
            step(v.memset(decay.rearrange("p h (b t) -> p (h b) t", t=T)[:, :, 0:1], 0.0))
            dve.wait_ge(S["ld_const"], 16)
            step(v.tensor_copy(id16[:], ident))
            step(v.tensor_copy(bsel[:], sel_batch.unsqueeze(2).to_broadcast([PARTS * NB, NB, P])))
            v.tensor_copy(sel[:], sel_rows.unsqueeze(2).to_broadcast([PARTS * G, 2 * NS, P])).then_inc(S["decay_zeroed"], 1)

            dve.wait_ge(S["mod_raw"], 2)
            m6 = mod.rearrange("p (k s d) -> p k s d", k=2, s=3)
            t6 = mod_t.rearrange("p (k s d) -> p k s d", k=2, s=3)
            step(v.tensor_scalar(m6[:, :, 1, :], m6[:, :, 1, :], 1.0, None, ALU.add))
            step(v.tensor_scalar(t6[:, :, 0, :], m6[:, :, 2, :], 0.0, 2.0, ALU.is_ge, ALU.mult))
            step(v.scalar_tensor_tensor(t6[:, :, 1, :], m6[:, :, 2, :], -1.0, m6[:, :, 2, :], ALU.mult, ALU.max))
            settle()
            step(v.tensor_scalar(t6[:, :, 1, :], t6[:, :, 1, :], 0.25, None, ALU.max))
            settle()
            step(v.scalar_tensor_tensor(m6[:, :, 2, :], t6[:, :, 0, :], -1.0, t6[:, :, 1, :], ALU.add, ALU.mult))
            settle()
            step(v.tensor_copy(mod_hi, mod))
            settle()
            step(v.scalar_tensor_tensor(mod_t, mod_hi, cut_m[:, 0:1], mod, ALU.mult, ALU.add))
            settle()
            step(v.tensor_copy(mod_hi, mod_t))
            settle()
            v.scalar_tensor_tensor(mod_parts, mod_hi, cut_m[:, 1:2], mod_t, ALU.mult, ALU.add
                                   ).then_inc(S["mod_parts_ok"], 1)
            dve.wait_ge(S["act_step"], 1)
            v.tensor_scalar(neg_a[:], neg_a[:], -1.0, None, ALU.mult).then_inc(S["neg_a_ok"], 1)
            for b in range(NB):
                dve.wait_ge(S["mod_bc_copied"], 2 * b + 2)
                v.tensor_copy(pay[:, 2 * b:2 * b + 2, 2 * D:3 * D],
                              side[1][:, D:2 * D].unsqueeze(1).to_broadcast([P, 2, D])).then_inc(S["gate_rows"], 1)

            def rows_of(c, section):
                r = mod_b[:, BC * c:BC * (c + 1), section * D:(section + 1) * D]
                return r.unsqueeze(2).to_broadcast([P, BC, TC // BC, D])

            def by_batch(t):
                return t.rearrange("p (b k) d -> p b k d", b=BC)

            def statistics(which, src, ready):
                for t in range(TC):
                    step(v.bn_stats(bn[:, which, t, :], src[:, t, :]))
                settle()
                for t in range(TC):
                    ins = v.bn_aggr(mv[:, which, t, :], bn[:, which, t, :])
                    if t < TC - 1:
                        step(ins)
                ins.then_inc(ready, 1)

            def standardise(which, src, dst):
                for t in range(TC):
                    step(v.tensor_scalar(dst[:, t, :], src[:, t, :], mv[:, which, t, 0:1],
                                         rs[:, 3 * which, t:t + 1], ALU.subtract, ALU.mult))
                settle()

            def square_sums(which, src, ready):
                for t in range(TC):
                    ins = v.scalar_tensor_tensor(hn[:, which, t, :], src[:, t, :], 1.0, src[:, t, :], ALU.mult, ALU.mult,
                                                 accum_out=ss[:, which, t:t + 1])
                    if t < TC - 1:
                        step(ins)
                ins.then_inc(ready, 1)

            def scaled(which, src, ready):
                for t in range(TC):
                    ins = v.tensor_scalar(hn[:, which, t, :], src[:, t, :], rs[:, 1 + which, t:t + 1], None, ALU.mult)
                    if t < TC - 1:
                        step(ins)
                ins.then_inc(ready, 1)

            def ln_stats(k):
                dve.wait_ge(S["ld_x"][k], 16)
                statistics(0, x[:, chunk(k), :], S["ln_var"])

            def ln_apply(k):
                hk = h[:, k % 4]
                dve.wait_ge(S["ln_var"], k + 1)
                dve.wait_ge(S["ln_rstd"], k + 1)
                standardise(0, x[:, chunk(k), :], hk)
                step(v.tensor_tensor(by_batch(hk), by_batch(hk), rows_of(k, CA), ALU.mult))
                settle()
                step(v.tensor_tensor(by_batch(hk), by_batch(hk), rows_of(k, SA), ALU.add))
                settle()
                if k:
                    dve.wait_ge(S["hn_tr"], k)
                square_sums(0, hk, S["rms_ss"])

            def rms_apply(k):
                dve.wait_ge(S["rms_rs"], k + 1)
                scaled(0, h[:, k % 4], S["hn_ok"])

            def other_taps(j):
                def stage(k):
                    dve.wait_ge(S["conv0"], NH * k + j + 1)
                    xm = side[j].rearrange("p (b t) -> p b t", b=BC)
                    acc = u[:, k % 2, j, :].rearrange("p (b t) -> p b t", b=BC)
                    for s in range(1, TAPS):
                        ins = v.scalar_tensor_tensor(acc[:, :, s:T], xm[:, :, 0:T - s],
                                                     chan[:, j, TAPS - 1 - s:TAPS - s], acc[:, :, s:T], ALU.mult, ALU.add)
                        if s < TAPS - 1:
                            step(ins)
                            settle()
                    ins.then_inc(S["conv_ok"], 1)
                return stage

            def first_rest(k):
                dve.wait_ge(S["dbc_copied"], k + 1)
                dve.wait_ge(S["dt_ok"], k + 1)
                v.scalar_tensor_tensor(dbc_t[:], dbc_hi[:], cut_g[:, 0:1], side[0][0:PARTS * G, :], ALU.mult, ALU.add
                                       ).then_inc(S["dbc_r1"], 1)

            def parts_of(k):
                dve.wait_ge(S["dbc_mid"], k + 1)
                v.scalar_tensor_tensor(dbc_parts[:, k % 2, :], dbc_hi[:], cut_g[:, 1:2], dbc_t[:], ALU.mult, ALU.add
                                       ).then_inc(S["dbc_ok"], 1)

            def positive_part(k):
                for j in range(NH):
                    dve.wait_ge(S["dp_mm"], NH * k + j + 1)
                    v.tensor_scalar(delta[:, k % 2, j, :], side[j], chan[:, j, TAPS + 1:TAPS + 2], 0.0, ALU.add, ALU.max
                                    ).then_inc(S["dp_max"], 1)

            def y_out(k):
                dve.wait_ge(S["summed"], STEPS * (k + 1))
                dve.wait_ge(S["z_ok"], NH * (k + 1))
                for j in range(NH):
                    ins = v.scalar_tensor_tensor(u[:, k % 2, j, :], u[:, k % 2, j, :], chan[:, j, TAPS + 2:TAPS + 3],
                                                 ysum[:, j, :], ALU.mult, ALU.add)
                    if j < NH - 1:
                        step(ins)
                ins.then_inc(S["y_read"], 1)

            def residual(k):
                hk = h[:, k % 4]
                dve.wait_ge(S["op_mm"], k + 1)
                v.tensor_tensor(hk, side[0].rearrange("p (t d) -> p t d", d=D), hk, ALU.add).then_inc(S["h2_ok"], 1)
                dve.wait_ge(S["h2_ok"], k + 1)
                if k:
                    dve.wait_ge(S["hn2_tr"], k)
                square_sums(1, hk, S["rms2_ss"])

            def rms2_apply(k):
                dve.wait_ge(S["rms2_rs"], k + 1)
                scaled(1, h[:, k % 4], S["hn2_ok"])

            def stream(k):
                hk = h[:, k % 4]
                dve.wait_ge(S["f2_mm"], k + 1)
                v.tensor_tensor(hk, side[1].rearrange("p (t d) -> p t d", d=D), hk, ALU.add).then_inc(S["f2_read"], 1)
                dve.wait_ge(S["f2_read"], k + 1)
                step(v.tensor_tensor(by_batch(hk), by_batch(hk), rows_of(k, GA), ALU.mult))
                settle()
                x1 = pay[:, chunk(k), D:2 * D]
                step(v.tensor_tensor(x1, hk, x[:, chunk(k), :], ALU.add))
                settle()
                statistics(1, x1, S["ln2_var"])

            def ln2_apply(k):
                hm = pay[:, chunk(k), 0:D]
                dve.wait_ge(S["ln2_var"], k + 1)
                dve.wait_ge(S["ln2_rstd"], k + 1)
                standardise(1, pay[:, chunk(k), D:2 * D], hm)
                step(v.tensor_tensor(by_batch(hm), by_batch(hm), rows_of(k, CB), ALU.mult))
                settle()
                v.tensor_tensor(by_batch(hm), by_batch(hm), rows_of(k, SB), ALU.add).then_inc(S["hm_ok"], 1)

            def keep_logits(k):
                dve.wait_ge(S["lg_mm"], k + 1)
                v.tensor_copy(logits[:, chunk(k), :], side[1][:, 0:TC * NE].rearrange("p (t e) -> p t e", e=NE)
                              ).then_inc(S["lg_ok"], 1)

            def scan_step(c, n):
                k = STEPS * c + n
                dve.wait_ge(S["drive_ok"], k + 1)
                if k >= 4:
                    dve.wait_ge(S["weighted"], k - 3)
                for j in range(NH):
                    dve.wait_ge(S["decay_ok"], NH * k + j + 1)
                    v.tensor_tensor_scan(state[:, n % 4, j * CH:(j + 1) * CH], decay[:, j, :],
                                         drive[:, n % 2, j * CH:(j + 1) * CH], 0.0, ALU.mult, ALU.add
                                         ).then_inc(S["scanned"], 1)

            def weight_step(c, n):
                k = STEPS * c + n
                dve.wait_ge(S["c_bcast"], k + 1)
                dve.wait_ge(S["scanned"], NH * (k + 1))
                if k >= 2:
                    dve.wait_ge(S["summed"], k - 1)
                v.tensor_tensor(part[:, n % 2, :].rearrange("p (h t) -> p h t", h=NH),
                                state[:, n % 4, :].rearrange("p (h t) -> p h t", h=NH),
                                bank_c.unsqueeze(1).to_broadcast([P, NH, CH]), ALU.mult).then_inc(S["weighted"], 1)

            beside = BESIDE(((LN_V, ln_stats, 1), (LNA_V, ln_apply, 1), (RMSA_V, rms_apply, 1),
                             (TAP0_V, other_taps(0), 1), (TAP1_V, other_taps(1), 1), (REST_V, first_rest, 1),
                             (PARTS_V, parts_of, 1), (POS_V, positive_part, 1),
                             (RES_V, residual, -1), (RMS2A_V, rms2_apply, -1),
                             (STREAM_V, stream, -2), (LN2A_V, ln2_apply, -2), (LG_V, keep_logits, -2)))
            ln_stats(0)
            dve.wait_ge(S["mod_bc_copied"], 2 * NB)
            ln_apply(0)
            rms_apply(0)
            other_taps(0)(0)
            other_taps(1)(0)
            first_rest(0)
            parts_of(0)
            positive_part(0)
            for c in range(NC):
                scan_step(c, 0)
                if c:
                    y_out(c - 1)
                for n in range(STEPS):
                    if n + 1 < STEPS:
                        scan_step(c, n + 1)
                    weight_step(c, n)
                    beside(c, n)
            y_out(NC - 1)
            stream(NC - 2)
            residual(NC - 1)
            ln2_apply(NC - 2)
            rms2_apply(NC - 1)
            keep_logits(NC - 2)
            stream(NC - 1)
            ln2_apply(NC - 1)
            keep_logits(NC - 1)

            def per_token(t):
                return t.unsqueeze(2).to_broadcast([P, NT, NE])

            dve.wait_ge(S["lg_ok"], NC)
            step(v.tensor_reduce(top[:], logits[:], AX_X, ALU.max))
            settle()
            v.tensor_tensor(sm, logits[:], per_token(top[:]), ALU.subtract).then_inc(S["e_d"], 1)
            dve.wait_ge(S["e_d"], 1)
            step(v.tensor_scalar(hot, sm, 0.0, None, ALU.is_equal))
            settle()
            step(v.tensor_tensor(hot, hot, prefer.unsqueeze(1).to_broadcast([P, NT, NE]), ALU.mult))
            settle()
            step(v.tensor_reduce(first[:], hot, AX_X, ALU.max))
            settle()
            step(v.tensor_tensor(hot, hot, per_token(first[:]), ALU.is_equal))
            settle()
            step(v.tensor_scalar(first[:], first[:], -float(CAP), float(CAP * NE), ALU.mult, ALU.add))
            dve.wait_ge(S["e_exp"], 1)
            step(v.tensor_reduce(top[:], msk, AX_X, ALU.add))
            settle()
            step(v.reciprocal(top[:], top[:]))
            settle()
            step(v.tensor_tensor(msk, hot, per_token(top[:]), ALU.mult))
            settle()
            step(v.scalar_tensor_tensor(msk, hot, -1.0, msk, ALU.add, ALU.add))
            settle()
            for k in range(PARTS):
                step(v.tensor_copy(h_parts[:, :, k, :], hot))
                step(v.tensor_copy(m_parts[:, :, k, :], msk))
                settle()
                if k < PARTS - 1:
                    step(v.tensor_tensor(msk, msk, m_parts[:, :, k, :], ALU.subtract))
                    settle()
            v.memset(junk2[:, 0, 0:1], 0.0).then_inc(S["parts_ok"], 1)
            dve.wait_ge(S["rt_tr"], 2 * NT)
            v.tensor_copy(m_rows, ps[0:PARTS * NE, 0:2, :].bitcast(BF16)).then_inc(S["hid_ok"], 1)
            for t in range(NT):
                dve.wait_ge(S["row_mm"], t + 1)
                row = ps[:, 4 * (t % 2):4 * (t % 2) + 4, :].rearrange("p b t -> p (b t)")
                mine = top[:, t:t + 1]
                if t >= 2:
                    dve.wait_ge(S["ranked"], t - 1)
                if t:
                    step(v.tensor_scalar(junk[:, t % 2, 0:t * P], row[:, 0:t * P], mine, None, ALU.is_ge, ALU.add,
                                         accum_out=cnt[:, t, 0:1]))
                else:
                    step(v.memset(cnt[:, 0, 0:1], 0.0))
                step(v.tensor_scalar(junk[:, t % 2, t * P:TOK], row[:, t * P:TOK], mine, None, ALU.is_gt, ALU.add,
                                     accum_out=cnt[:, t, 1:2]))
                v.scalar_tensor_tensor(junk2[:, t % 2, :], row[:, t * P:(t + 1) * P], mine, earlier, ALU.is_equal, ALU.mult,
                                       accum_out=cnt[:, t, 2:3]).then_inc(S["ranked"], 1)

            for s in range(0, ST, 4):
                g = s // 4
                dve.wait_ge(S["xt_tr"], g + 1)
                v.tensor_copy(xe_t[:, s * P:(s + 4) * P], ps[:, g % 2, :]).then_inc(S["xt_ok"], 1)
            done = 0
            for e in range(NE):
                dve.wait_ge(S["e2_mm"], e + 1)
                v.tensor_scalar(o_t[:, e * CAP:(e + 1) * CAP], ps[:, 4 + e % 2, 0:CAP],
                                cols[:, 2 + FB + 2 * NE + e:3 + FB + 2 * NE + e], None, ALU.add).then_inc(S["e2_ok"], 1)
                while (done + 4) * P <= (e + 1) * CAP:
                    g = done // 4
                    dve.wait_ge(S["o_tr"], g + 1)
                    f = fin[:, done:done + 4, :]
                    step(v.tensor_tensor(f, ps[:, 6 + g % 2, :].rearrange("p (s d) -> p s d", d=D),
                                         xe[:, done:done + 4, 2 * D:3 * D], ALU.mult))
                    settle()
                    v.tensor_tensor(f, f, xe[:, done:done + 4, D:2 * D], ALU.add).then_inc(S["fin_ok"], 1)
                    done += 4

        @block.tensor
        def _(pe):
            mm = nc.tensor.matmul
            pe.wait_ge(S["silu_c_ok"], 1)
            mm(side[0][0:PARTS * NB, :], silu_c[:], w_mod[:, 0:CH], start=True, stop=True).then_inc(S["mod_mm"], 1)
            mm(side[1][0:PARTS * NB, 0:6 * D - CH], silu_c[:], w_mod[:, CH:6 * D], start=True, stop=True
               ).then_inc(S["mod_mm"], 1)
            pe.wait_ge(S["mod_parts_ok"], 1)
            for b in range(NB):
                if b:
                    pe.wait_ge(S["mod_bc_copied"], 2 * b)
                    pe.wait_ge(S["gate_rows"], b)
                mm(side[0], bsel[:, b, :], mod_parts[:, 0:CH], start=True, stop=True).then_inc(S["mod_bc"], 1)
                mm(side[1][:, 0:6 * D - CH], bsel[:, b, :], mod_parts[:, CH:6 * D], start=True, stop=True
                   ).then_inc(S["mod_bc"], 1)

            def to_channels(bank, src, done):
                for t in range(TC):
                    ins = nc.tensor.transpose(bank[:, t * P:(t + 1) * P], src[:, t, :], ident)
                ins.then_inc(done, 1)

            def hn_to_channels(k):
                pe.wait_ge(S["hn_ok"], k + 1)
                if k == 0:
                    pe.wait_ge(S["gate_rows"], NB)
                    pe.wait_ge(S["mod_bc_copied"], 2 * NB)
                else:
                    pe.wait_ge(S["dp_abs"], NH * k)
                if k >= 2:
                    pe.wait_ge(S["h2_ok"], k - 1)
                to_channels(side[0], hn[:, 0], S["hn_tr"])

            def in_proj_x(k):
                pe.wait_ge(S["h_t_ok"], k + 1)
                pe.wait_ge(S["ld_w"], 16 * 5)
                if k >= 2:
                    pe.wait_ge(S["h2_t_ok"], k - 1)
                for j in range(NH):
                    mm(side[j], w_in[:, j * P:(j + 1) * P], h_t[:, 0, :], start=True, stop=True).then_inc(S["xm_mm"], 1)

            def in_proj_z(k):
                for j in range(NH):
                    pe.wait_ge(S["conv_ok"], NH * k + j + 1)
                    mm(side[j], w_in[:, DI + j * P:DI + (j + 1) * P], h_t[:, 0, :], start=True, stop=True
                       ).then_inc(S["z_mm"], 1)

            def x_proj(k):
                pe.wait_ge(S["u_ok"], NH * (k + 1))
                pe.wait_ge(S["z_ok"], NH * k + 1)
                for j in range(NH):
                    ins = mm(side[0][0:PARTS * G, :], w_xp[:, j, :], u[:, k % 2, j, :], start=(j == 0), stop=(j == NH - 1))
                ins.then_inc(S["dbc_mm"], 1)

            def dt_proj(k):
                pe.wait_ge(S["dt_ok"], k + 1)
                pe.wait_ge(S["z_ok"], NH * (k + 1))
                pe.wait_ge(S["dbc_r1"], k + 1)
                if k >= 2:
                    pe.wait_ge(S["gelu_ok"], FB * (k - 1))
                for j in range(NH):
                    mm(side[j], w_dt[:, j * P:(j + 1) * P], dt_rows[:], start=True, stop=True).then_inc(S["dp_mm"], 1)

            def out_proj(k):
                if k == 0:
                    pe.wait_ge(S["ld_m"], 16 * 5)
                pe.wait_ge(S["yg_ok"], k + 1)
                pe.wait_ge(S["dp_abs"], NH * min(k + 2, NC))
                for t in range(TC):
                    for j in range(NH):
                        ins = mm(side[0][:, t * D:(t + 1) * D], u[:, k % 2, j, t * P:(t + 1) * P], w_out[:, j, :],
                                 start=(j == 0), stop=(j == NH - 1))
                ins.then_inc(S["op_mm"], 1)

            def hn2_to_channels(k):
                pe.wait_ge(S["hn2_ok"], k + 1)
                if k:
                    pe.wait_ge(S["lg_ok"], k)
                to_channels(side[1], hn[:, 1], S["hn2_tr"])

            def mlp_up(k):
                pe.wait_ge(S["h2_t_ok"], k + 1)
                pe.wait_ge(S["z_ok"], NH * min(k + 3, NC))
                for f in range(FB):
                    if f == 1:
                        pe.wait_ge(S["dbc_r1"], min(k + 3, NC))
                        pe.wait_ge(S["dt_ok"], min(k + 3, NC))
                    if f >= 2:
                        pe.wait_ge(S["gelu_ok"], FB * k + f - 1)
                    mm(side[1 - f % 2], w_m1[:, f * P:(f + 1) * P], h_t[:, 1, :], start=True, stop=True
                       ).then_inc(S["f1_mm"], 1)

            def mlp_down(k):
                pe.wait_ge(S["sel_ok"], 1)
                pe.wait_ge(S["gelu_ok"], FB * (k + 1))
                pe.wait_ge(S["dp_abs"], NH * min(k + 3, NC))
                for t in range(TC):
                    mm(side[1][:, t * D:(t + 1) * D], ones[:], b2row[:], start=True, stop=False)
                    for f in range(FB):
                        ins = mm(side[1][:, t * D:(t + 1) * D], m_t[:, f, t * P:(t + 1) * P], w_m2[:, f, :],
                                 start=False, stop=(f == FB - 1))
                ins.then_inc(S["f2_mm"], 1)

            def hm_to_channels(k):
                pe.wait_ge(S["hm_ok"], k + 1)
                pe.wait_ge(S["f2_read"], k + 1)
                to_channels(side[1], pay[:, chunk(k), 0:D], S["hm_tr"])

            def gate_logits(k):
                pe.wait_ge(S["hm_t_ok"], k + 1)
                for t in range(TC):
                    ins = mm(side[1][:, t * NE:(t + 1) * NE], h_t[:, 1, t * P:(t + 1) * P], w_g[:], start=True, stop=True)
                ins.then_inc(S["lg_mm"], 1)

            def bcast_b(c, n):
                k = STEPS * c + n
                if k:
                    pe.wait_ge(S["b_copied"], k)
                mm(bank_b, sel[:, n, :], dbc_parts[:, c % 2, :], start=True, stop=True).then_inc(S["b_bcast"], 1)

            def bcast_c(c, n):
                k = STEPS * c + n
                if k:
                    pe.wait_ge(S["weighted"], k)
                mm(bank_c, sel[:, NS + n, :], dbc_parts[:, c % 2, :], start=True, stop=True).then_inc(S["c_bcast"], 1)

            def sum_step(c, n):
                k = STEPS * c + n
                pe.wait_ge(S["weighted"], k + 1)
                if c and n == 0:
                    pe.wait_ge(S["y_read"], c)
                for j in range(NH):
                    ins = mm(ysum[:, j, :], ident, part[:, n % 2, j * CH:(j + 1) * CH], start=(n == 0), stop=(n == STEPS - 1),
                             skip_group_check=True)
                ins.then_inc(S["summed"], 1)

            beside = BESIDE(((TR_T, hn_to_channels, 1), (XM_T, in_proj_x, 1), (Z_T, in_proj_z, 1), (XP_T, x_proj, 1),
                             (DT_T, dt_proj, 1), (OP_T, out_proj, -1), (TR2_T, hn2_to_channels, -1),
                             (UP_T, mlp_up, -1), (DOWN_T, mlp_down, -2), (TR3_T, hm_to_channels, -2),
                             (LG_T, gate_logits, -2)))
            hn_to_channels(0)
            in_proj_x(0)
            in_proj_z(0)
            x_proj(0)
            dt_proj(0)
            for c in range(NC):
                pe.wait_ge(S["dbc_ok"], c + 1)
                for n in range(4):
                    bcast_b(c, n)
                    if n == 0:
                        bcast_c(c, 0)
                for n in range(STEPS):
                    if n + 4 < STEPS:
                        bcast_b(c, n + 4)
                    if n + 1 < STEPS:
                        bcast_c(c, n + 1)
                    sum_step(c, n)
                    beside(c, n)
            mlp_down(NC - 2)
            out_proj(NC - 1)
            hm_to_channels(NC - 2)
            gate_logits(NC - 2)
            hn2_to_channels(NC - 1)
            mlp_up(NC - 1)
            mlp_down(NC - 1)
            hm_to_channels(NC - 1)
            gate_logits(NC - 1)

            pe.wait_ge(S["parts_ok"], 1)
            ps16 = ps[:, 0:4, :].bitcast(BF16)
            for k, src in enumerate((m_parts, h_parts)):
                for t in range(NT):
                    half_bank = ps16[0:PARTS * NE, 2 * k + t // 8, (t % 8) * P:(t % 8 + 1) * P]
                    nc.tensor.transpose(half_bank, src[:, t, :, :].rearrange("p k e -> p (k e)"), id16[:]
                                        ).then_inc(S["rt_tr"], 1)
            pe.wait_ge(S["rt_rows"], 1)
            pe.wait_ge(S["hid_ok"], 1)
            for t in range(NT):
                if t >= 2:
                    pe.wait_ge(S["ranked"], t - 1)
                for b in range(4):
                    ins = mm(ps[:, 4 * (t % 2) + b, :], h_rows[:, t * P:(t + 1) * P], m_rows[:, b * CH:(b + 1) * CH],
                             start=True, stop=True)
                ins.then_inc(S["row_mm"], 1)

            pe.wait_ge(S["ld_e"], 32)
            pe.wait_ge(S["ranked"], NT)
            pe.wait_ge(S["xe_in"], 16 * (ST // 4))
            for g in range(ST // 4):
                if g >= 2:
                    pe.wait_ge(S["xt_ok"], g - 1)
                for s in range(4):
                    ins = nc.tensor.transpose(ps[:, g % 2, s * P:(s + 1) * P], xe[:, 4 * g + s, 0:D], ident)
                ins.then_inc(S["xt_tr"], 1)

            def up(e):
                pe.wait_ge(S["xt_ok"], -(-(e + 1) * CAP // CH))
                if e >= 2:
                    pe.wait_ge(S["e1_ok"], 2 * (e - 1))
                for j in range(2):
                    ins = mm(ps[:, 2 + e % 2, j * CAP:(j + 1) * CAP], w_e1[:, e, j * P:(j + 1) * P],
                             xe_t[:, e * CAP:(e + 1) * CAP], start=True, stop=True)
                ins.then_inc(S["e1_mm"], 1)

            def down(e):
                pe.wait_ge(S["e1_ok"], 2 * (e + 1))
                if e >= 2:
                    pe.wait_ge(S["e2_ok"], e - 1)
                for j in range(2):
                    ins = mm(ps[:, 4 + e % 2, 0:CAP], w_e2[:, e, j, :], g_t[:, e % 2, j, :], start=(j == 0), stop=(j == 1))
                ins.then_inc(S["e2_mm"], 1)

            def to_slots(g):
                pe.wait_ge(S["e2_ok"], -(-(g + 1) * CH // CAP))
                if g >= 2:
                    pe.wait_ge(S["fin_ok"], g - 1)
                for s in range(4):
                    ins = nc.tensor.transpose(ps[:, 6 + g % 2, s * P:(s + 1) * P],
                                              o_t[:, (4 * g + s) * P:(4 * g + s + 1) * P], ident)
                ins.then_inc(S["o_tr"], 1)

            up(0)
            g = 0
            for e in range(NE):
                if e + 1 < NE:
                    up(e + 1)
                down(e)
                while (g + 1) * CH <= e * CAP:
                    to_slots(g)
                    g += 1
            while g < SLOTS // CH:
                to_slots(g)
                g += 1


def kernel(**inputs):
    import numpy as np
    import concourse.bacc as bacc
    from concourse.bass_utils import run_bass_kernel_spmd as run

    def arr(n):
        return np.asarray(inputs["L0_" + n])

    def lay(v):
        return np.ascontiguousarray(v)

    def by_part(v, parts):
        return lay(v.reshape(parts, P, -1).transpose(1, 0, 2))

    f = np.float32
    consts = np.zeros((P, 3 * P + 2 * NS + 64), f)
    consts[:, 0:P] = np.eye(P)
    consts[:, P:2 * P] = np.tril(np.ones((P, P)), -1)
    consts[:, 2 * P:2 * P + NT] = np.arange(P)[:, None] + P * np.arange(NT)[None, :] + 1
    consts[:, 2 * P + NT:2 * P + NT + NE] = NE - np.arange(NE)[None, :]
    o = 2 * P + NT + NE
    for k in range(PARTS):
        for n in range(2 * NS):
            consts[k * G + RANK + n, o + n] = 1
        for b in range(NB):
            consts[k * NB + b, o + 2 * NS + b] = 1
    o += 2 * NS + NB
    consts[G:PARTS * G, o] = -1
    consts[2 * G:PARTS * G, o + 1] = -1
    consts[NB:PARTS * NB, o + 2] = -1
    consts[2 * NB:PARTS * NB, o + 3] = -1
    consts[:, o + 4:o + 4 + TC] = -0.5

    x_proj = arr("attn_x_proj_w").T
    chan = np.concatenate([arr("attn_conv_w")[:, 0, :], arr("attn_conv_b")[:, None], arr("attn_dt_proj_b")[:, None],
                           arr("attn_D")[:, None], arr("attn_A_log")], 1)
    cols = np.concatenate([arr("attn_norm1_w")[:, None], arr("attn_norm2_w")[:, None],
                           arr("attn_mlp_b1").reshape(FB, P).T, arr("ffn_b1").reshape(NE * 2, P).T,
                           arr("ffn_b2").T], 1)
    arrays = {
        "x": lay(arr("attn_x").reshape(NT, P, D).transpose(1, 0, 2)),
        "c_t": lay(np.concatenate([arr("c").T] * PARTS, 1)),
        "w_mod": lay(arr("wmod")),
        "consts": consts,
        "cols": lay(cols),
        "chan": by_part(chan, NH),
        "w_in": lay(arr("attn_in_proj_w").T),
        "w_xp": by_part(np.concatenate([x_proj] * PARTS, 1), NH),
        "w_dt": lay(arr("attn_dt_proj_w").T),
        "w_out": by_part(arr("attn_out_proj_w").T, NH),
        "w_m1": lay(arr("attn_mlp_w1").T),
        "w_m2": by_part(arr("attn_mlp_w2").T, FB),
        "b2row": lay(arr("attn_mlp_b2")[None, :]),
        "w_g": lay(arr("ffn_Wg")),
        "w_e1": lay(arr("ffn_W1").transpose(1, 0, 2)),
        "w_e2": lay(arr("ffn_W2").reshape(NE, H // P, P, D).transpose(2, 0, 1, 3)),
    }
    nc = bacc.Bacc("TRN2", target_bir_lowering=False, num_devices=1)
    a = {n: nc.dram_tensor("in_" + n, v.shape, F32, kind="ExternalInput").ap() for n, v in arrays.items()}
    out = nc.dram_tensor("out_0", (NB, T, D), F32, kind="ExternalOutput").ap()
    xe_dram = nc.dram_tensor("xe_rows", (SLOTS, W_PAY), F32, kind="Internal").ap()
    adaln_mamba_moe(nc, a, out, xe_dram, None)
    r = run(nc, [{"in_" + n: v for n, v in arrays.items()}], core_ids=[0])
    return r.results[0]["out_0"]
```

```python
from contextlib import ExitStack

import concourse.bass as bass
from concourse import mybir

F32 = mybir.dt.float32
BF16 = mybir.dt.bfloat16
U32 = mybir.dt.uint32
ALU = mybir.AluOpType
ACT = mybir.ActivationFunctionType
AX_X = mybir.AxisListType.X

P = 128
NB, T = 8, 256
D = 128
DI = 2 * D
NH = DI // P
NS = 16
RANK = D // 16
TAPS = 4
F = 4 * D
FB = F // P
TOK = NB * T
NT = TOK // P
CH = 512
NC = TOK // CH
TC = CH // P
BC = CH // T
NE, H = 16, 256
CAP = -(-5 * TOK // (4 * NE))
SLOTS = NE * CAP
ST = SLOTS // P
G = RANK + 2 * NS
PARTS = 3
W_PAY = 3 * D + 1
SA, CA, GA, SB, CB, GB = range(6)
FAR = 8192.0
STEPS = NS
EARLY = NT - TC
COUNTS = 2 + -(-EARLY // TC)
B_SENT, B_COPIED = 4, 2


AT = {
    "LN_V": (-99, -67, 2, 13),
    "LN_P": (-99, -50, 7, 21),
    "LNA_V": (-95, -1, 5, 24),
    "RMS_P": (-86, -7, 9, 34),
    "TR_T": (-96, 0, 17, 35),
    "HT_A": (-68, 3, 19, 38),
    "XM0_T": (-94, 1, 20, 37),
    "XM1_T": (-92, 2, 21, 39),
    "TAP0_A": (-67, 4, 23, 41),
    "TAP1_A": (-62, 5, 24, 43),
    "TAP0_V": (-71, 3, 22, 41),
    "TAP1_V": (-45, 4, 23, 42),
    "SILU0_A": (-60, 6, 25, 44),
    "SILU1_A": (-49, 6, 25, 44),
    "Z0_T": (-68, 4, 23, 41),
    "Z1_T": (-56, 4, 23, 42),
    "SZ0_A": (-59, 6, 25, 44),
    "SZ1_A": (-49, 6, 25, 44),
    "XP_T": (-51, 4, 23, 42),
    "PART1_A": (-46, 7, 25, 44),
    "REST_V": (-40, 6, 24, 43),
    "PART2_A": (-46, 8, 25, 44),
    "PARTS_V": (-39, 7, 24, 43),
    "DT0_T": (-21, 6, 23, 43),
    "DT1_T": (-3, 8, 26, 43),
    "POS0_V": (-7, 8, 24, 43),
    "POS1_V": (-5, 10, 27, 43),
    "ABS0_A": (-43, 12, 26, 45),
    "ABS1_A": (-33, 12, 29, 45),
    "SOFT_A": (-23, 13, 29, 46),
    "DELTA_P": (-40, 14, 30, 47),
    "DU_P": (-16, 15, 31, 47),
    "Y_V": (16, 31, 48, 63),
    "GATE_P": (18, 34, 51, 65),
    "OP0_T": (16, 32, 50, 67),
    "OP1_T": (16, 32, 50, 68),
    "RES_V": (17, 33, 52, 65),
    "RMS2_P": (20, 36, 55, 68),
    "TR2_T": (17, 36, 54, 71),
    "H2T_A": (23, 38, 57, 71),
    "UP0_T": (28, 44, 56, 72),
    "UP1_T": (28, 44, 57, 73),
    "GELU0_A": (31, 48, 59, 73),
    "GELU1_A": (31, 48, 64, 74),
    "UP2_T": (30, 46, 63, 74),
    "UP3_T": (30, 46, 64, 75),
    "GELU2_A": (32, 49, 65, 75),
    "GELU3_A": (32, 49, 67, 77),
    "DOWN0_T": (31, 47, 65, 77),
    "DOWN1_T": (31, 49, 66, 79),
    "STREAM_V": (32, 54, 64, 72),
    "LN2_P": (37, 57, 67, 70),
    "LN2A_V": (36, 56, 66, 73),
    "STAY_P": (64, 66, 69, 71),
    "TR3_T": (36, 58, 69, 85),
    "HMT_A": (38, 61, 70, 79),
    "LG_T": (36, 59, 70, 86),
    "LG_V": (38, 61, 67, 77),
    "SQ_A": (-79, -24, 8, 28),
    "RMSA_A": (-70, -19, 16, 33),
    "SQ2_A": (19, 35, 54, 68),
    "RMS2A_A": (19, 36, 56, 69),
    "MB_T": (-97, -75, -67, 31),
    "MB_A": (-67, -61, -32, 66),
    "GB_P": (-87, -64, -28, -25),
    "R_CHOOSE_V": (68,),
    "R_EXP_A": (72,),
    "R_SPLIT_V": (69,),
    "R_TR_T": (76,),
    "R_ROWS_A": (78,),
    "R_VALUES_V": (70,),
    "R_CMP_V": (71, 75, 81, 84),
    "R_VAL_T": (78, 82, 87, 90),
    "R_EXP2_A": (80,),
    "R_ROWS2_A": (81,),
    "R_CHOOSE2_V": (78,),
    "R_SPLIT2_V": (79,),
    "R_VALUES2_V": (82,),
    "R_TR2_T": (89,),
    "R_BEF_T": (83, 88, 92, 93),
}


def BESIDE(*stages):
    at = {}
    for name, stage in stages:
        for k, step in enumerate(AT[name]):
            at.setdefault(step, []).append((k, stage))
    def run(first, last):
        for step in sorted(at):
            if first <= step <= last:
                for k, stage in at[step]:
                    stage(k)
    return run


def adaln_mamba_moe(nc, a, out, xe_dram):
    with ExitStack() as ctx:
        def sb(name, shape, dt=F32):
            return ctx.enter_context(nc.sbuf_tensor(name, shape, dt))

        def sem(name):
            return ctx.enter_context(nc.semaphore(name))

        x = sb("x", [P, NT, D])
        w_in = sb("w_in", [D, 2 * DI])
        w_xp = sb("w_xp", [P, NH, PARTS * G])
        w_dt = sb("w_dt", [RANK, DI])
        w_out = sb("w_out", [P, NH, D])
        w_m1 = sb("w_m1", [D, F])
        w_m2 = sb("w_m2", [P, FB, D])
        w_g = sb("w_g", [D, NE])
        chan = sb("chan", [P, NH, TAPS + 3 + NS])
        cols = sb("cols", [P, 2 + FB + 2 * NE + NE])
        b2row = sb("b2row", [1, D])
        c_t = sb("c_t", [D, PARTS * NB])
        w_mod = sb("w_mod", [D, 6 * D])
        consts = sb("consts", [P, 3 * P + 2 * NS + 64])
        ident = consts[:, 0:P]
        earlier = consts[:, P:2 * P]
        token1 = consts[:, 2 * P:2 * P + NT]
        prefer = consts[:, 2 * P + NT:2 * P + NT + NE]
        o_ = 2 * P + NT + NE
        sel_rows = consts[0:PARTS * G, o_:o_ + 2 * NS]
        o_ += 2 * NS
        sel_batch = consts[0:PARTS * NB, o_:o_ + NB]
        o_ += NB
        cut_g = consts[0:PARTS * G, o_:o_ + 2]
        cut_m = consts[0:PARTS * NB, o_ + 2:o_ + 4]
        half = consts[:, o_ + 4:o_ + 4 + TC]
        ones = sb("ones", [1, P])
        id16 = sb("id16", [P, P], BF16)
        sel = sb("sel", [PARTS * G, 2 * NS, P], BF16)
        bsel = sb("bsel", [PARTS * NB, NB, P], BF16)
        neg_a = sb("neg_a", [P, NH, NS])

        silu_c = sb("silu_c", [D, PARTS * NB])
        mod_b = sb("mod_b", [P, NB, 6 * D])

        bn = sb("bn", [P, 2, TC, 6])
        mv = sb("mv", [P, 2, TC, 2])
        ss = sb("ss", [P, 2, TC])
        rs = sb("rs", [P, 4, TC])

        h = sb("h", [P, 4, TC, D])
        hn = sb("hn", [P, 2, TC, D])
        h_t = sb("h_t", [D, 3, CH])
        pay = sb("pay", [P, NT, W_PAY])
        base = sb("base", [P, TC, D])
        logits = sb("logits", [P, NT, NE])

        ARENA = 24576
        arena = sb("arena", [P, ARENA])
        at = [0]

        def take(n):
            at[0] += n
            assert at[0] <= ARENA, at[0]
            return arena[:, at[0] - n:at[0]]

        def halves(k):
            return take(k * NH * CH).rearrange("p (k h t) -> p k h t", k=k, h=NH)

        u, zg, delta, du = halves(2), halves(2), halves(2), halves(2)
        soft = take(NH * CH).rearrange("p (h t) -> p h t", h=NH)
        b_rows = take(4 * CH).rearrange("p (k t) -> p k t", k=4)
        drive = take(2 * NH * CH).rearrange("p (k t) -> p k t", k=2)
        state = take(4 * NH * CH).rearrange("p (k t) -> p k t", k=4)
        part = take(2 * NH * CH).rearrange("p (k t) -> p k t", k=2)
        m_t = take(FB * CH).rearrange("p (f t) -> p f t", f=FB)
        m_ = state.rearrange("p k t -> p (k t)")[0:PARTS * NB, :]
        mod, mod_t = m_[:, 0:6 * D], m_[:, 6 * D:12 * D]
        mod_hi = m_[:, 12 * D:15 * D].bitcast(BF16)
        mod_parts = m_[:, 15 * D:18 * D].bitcast(BF16)
        at[0] = 0
        xe = take(ST * W_PAY).rearrange("p (s w) -> p s w", w=W_PAY)
        xe_t = take(SLOTS)
        o_t = take(SLOTS)
        fin = take(SLOTS).rearrange("p (s d) -> p s d", d=D)
        g_t = take(2 * 2 * CAP).rearrange("p (k h s) -> p k h s", k=2, h=2)
        w_e1 = take(NE * H).rearrange("p (e h) -> p e h", e=NE)
        w_e2 = take(NE * H).rearrange("p (e k d) -> p e k d", e=NE, k=H // P)
        dbc_hi = sb("dbc_hi", [PARTS * G, CH], BF16)
        dbc_t = sb("dbc_t", [PARTS * G, CH])
        dbc_parts = sb("dbc_parts", [PARTS * G, 2, CH], BF16)
        dt_rows = sb("dt_rows", [RANK, CH])

        at[0] = 0
        h_rows = take(TOK // 2)[0:PARTS * NE, :].bitcast(BF16)
        at[0] = 2 * NH * CH
        m_rows = take(TOK // 2)[0:PARTS * NE, :].bitcast(BF16)
        at[0] = 4 * NH * CH
        sm = take(NT * NE).rearrange("p (t e) -> p t e", e=NE)
        hot = take(NT * NE).rearrange("p (t e) -> p t e", e=NE)
        msk = take(NT * NE).rearrange("p (t e) -> p t e", e=NE)
        m_parts = take(NT * PARTS * NE // 2).bitcast(BF16).rearrange("p (t k e) -> p t k e", k=PARTS, e=NE)
        h_parts = take(NT * PARTS * NE // 2).bitcast(BF16).rearrange("p (t k e) -> p t k e", k=PARTS, e=NE)
        greater = [take((NT - t) * P // 2).bitcast(BF16) for t in range(NT)]
        equal = take(2 * P).rearrange("p (k t) -> p k t", k=2)
        assert at[0] <= ST * W_PAY + 3 * SLOTS + 4 * CAP
        hot_t = x[:].rearrange("p t d -> p (t d)")[0:NE, :]
        top = sb("top", [P, NT])
        first = sb("first", [P, NT])
        cnt = sb("cnt", [P, COUNTS, NT])
        rank = sb("rank", [P, NT])
        slot_f = sb("slot_f", [P, 2, NT])
        minus16 = sb("minus16", [P, 2], BF16)
        tiles_before = sb("tiles_before", [NE, 2, NT])
        counted = sb("counted", [P, EARLY])
        ones_e = sb("ones_e", [NE, NT])
        slot = sb("slot", [P, NT], U32)
        tok_f = sb("tok_f", [P, ST, 2])
        tok = sb("tok", [P, ST], U32)
        zeros = m_t.rearrange("p f t -> p (f t)")[:, 0:4 * W_PAY]

        ps = ctx.enter_context(nc.psum_tensor("ps", [P, 8, CH], F32))
        bank_b, bank_c = ps[:, 0, :], ps[:, 1, :]
        decay = ps[:, 2:4, :]
        ysum = ps[:, 4:6, :]
        side = [ps[:, 6, :], ps[:, 7, :]]

        block = ctx.enter_context(nc.Block())
        S = {n: sem(n) for n in (
            "ld_mod", "ld_const", "ld_w", "ld_m", "ld_e", "dram_zeroed", "base_out", "rows_out", "final_out",
            "silu_c_ok", "mod_mm", "mod_raw", "mod_parts_ok", "mod_bc", "mod_bc_copied",
            "gate_rows", "ones_ok", "bsel_ok", "sel_ok", "h_ok", "decay_zeroed", "neg_a_ok",
            "ln_var", "ln_rstd", "rms_ss", "rms_rs", "hn_ok", "hn_tr", "h_t_ok",
            "xm_mm", "conv0", "conv_ok", "u_ok", "z_mm", "z_ok", "dbc_mm", "dbc_copied", "dbc_r1", "dbc_mid", "dbc_ok",
            "dt_ok", "dp_mm", "dp_abs", "dp_max", "dp_exp", "dp_ln", "delta_ok", "du_ok",
            "b_bcast", "b_copied", "drive_ok", "decay_ok", "scanned", "c_bcast", "weighted", "summed",
            "y_read", "yg_ok", "op_mm", "h2_ok", "rms2_ss", "rms2_rs", "hn2_ok", "hn2_tr", "h2_t_ok", "f1_mm", "gelu_ok",
            "f2_mm", "f2_read", "ln2_var", "ln2_rstd", "hm_ok", "hm_tr", "hm_t_ok", "lg_mm", "lg_ok", "base_ok",
            "e_exp", "e_d", "parts_ok", "m_rows_ok", "rt_tr", "h_rows_ok", "hot_t_ok", "counts_mm", "prefix_ok",
            "row_mm", "compared", "before_mm", "rank_ok", "slot_ok", "zero_ok", "xe_rest",
            "xt_tr", "xt_ok", "e1_mm", "e1_ok", "e2_mm", "e2_ok", "o_tr", "fin_ok",
            "dve_step", "act_step", "pool_step")}
        S["ld_x"] = [sem(f"ld_x{c}") for c in range(NC)]
        S["xe_hm"] = [sem(f"xe_hm{g}") for g in range(ST // 4)]

        unit_a = [(t, i, min(i + TC, EARLY)) for t in range(EARLY) for i in range(t, EARLY, TC)]
        units = unit_a + [(t, max(t, EARLY), NT) for t in range(NT)]
        GROUPS = ((0, 1), (1, 5), (5, EARLY), (EARLY, NT))
        OUT = [(0, 2), (2, 4)] + [(s, s + 4) for s in range(4, ST - 4, 4)] + [(ST - 4, ST - 2), (ST - 2, ST)]

        def last_unit(t):
            return len(unit_a) + t + 1

        def expert_rows(which, a):
            banks = slice(2 * which, 2 * which + 2) if a == 0 else slice(6 + which, 7 + which)
            return ps[0:PARTS * NE, banks, :].bitcast(BF16).rearrange("p b t -> p (b t)")

        def unit_bank(q, n):
            return ps[:, (0, 1, 2, 3, 5)[q % 5], 0:n]

        def chunk(c):
            return slice(TC * c, TC * (c + 1))

        @block.sync
        def _(sp):
            sp.dma_start(c_t[:], a["c_t"]).then_inc(S["ld_mod"], 16)
            sp.dma_start(w_mod[:], a["w_mod"]).then_inc(S["ld_mod"], 16)
            sp.dma_start(consts[:], a["consts"]).then_inc(S["ld_const"], 16)
            for c in range(NC):
                sp.dma_start(x[:, chunk(c), :], a["x"][:, chunk(c), :]).then_inc(S["ld_x"][c], 16)
                if c == 0:
                    sp.dma_start(cols[:], a["cols"]).then_inc(S["ld_w"], 16)
                    sp.dma_start(chan[:], a["chan"]).then_inc(S["ld_w"], 16)
                    sp.dma_start(w_in[:], a["w_in"]).then_inc(S["ld_w"], 16)
                    sp.dma_start(w_xp[:], a["w_xp"]).then_inc(S["ld_w"], 16)
                    sp.dma_start(w_dt[:], a["w_dt"]).then_inc(S["ld_w"], 16)
            sp.dma_start(w_out[:], a["w_out"]).then_inc(S["ld_m"], 16)
            sp.dma_start(w_m1[:], a["w_m1"]).then_inc(S["ld_m"], 16)
            sp.dma_start(w_m2[:], a["w_m2"]).then_inc(S["ld_m"], 16)
            sp.dma_start(b2row[:], a["b2row"]).then_inc(S["ld_m"], 16)
            sp.dma_start(w_g[:], a["w_g"]).then_inc(S["ld_m"], 16)
            sp.wait_ge(S["zero_ok"], 1)
            rows = xe_dram.rearrange("(p s) w -> p (s w)", p=P)
            for s in range(0, ST, 4):
                sp.dma_start(rows[:, s * W_PAY:(s + 4) * W_PAY], zeros).then_inc(S["dram_zeroed"], 16)
            ov = out.rearrange("b (t p) d -> p (b t) d", p=P)
            for c in range(NC):
                sp.wait_ge(S["base_ok"], c + 1)
                sp.dma_start(ov[:, chunk(c), :], base[:]).then_inc(S["base_out"], 16)
            sp.dma_start(w_e1, a["w_e1"]).then_inc(S["ld_e"], 16)
            sp.dma_start(w_e2, a["w_e2"]).then_inc(S["ld_e"], 16)
            sp.wait_ge(S["rows_out"], 16 * NT)
            xv = xe_dram.rearrange("(s p) w -> p s w", p=P)
            for g in range(ST // 4):
                s = slice(4 * g, 4 * g + 4)
                sp.dma_start(xe[:, s, 0:D], xv[:, s, 0:D]).then_inc(S["xe_hm"][g], 16)
            for g in range(ST // 4):
                s = slice(4 * g, 4 * g + 4)
                sp.dma_start(xe[:, s, D:W_PAY], xv[:, s, D:W_PAY]).then_inc(S["xe_rest"], 16)
            sp.wait_ge(S["base_out"], 16 * NC)
            sp.wait_ge(S["final_out"], 16 * ST)

        @block.gpsimd
        def _(gp):
            n_step = [0]

            def step(ins):
                n_step[0] += 1
                ins.then_inc(S["pool_step"], 1)

            def settle():
                gp.wait_ge(S["pool_step"], n_step[0])

            nc.gpsimd.memset(zeros, 0.0).then_inc(S["zero_ok"], 1)
            nc.gpsimd.memset(ones[:], 1.0).then_inc(S["ones_ok"], 1)
            gp.wait_ge(S["ld_const"], 16)
            nc.gpsimd.tensor_copy(bsel[:], sel_batch.unsqueeze(2).to_broadcast([PARTS * NB, NB, P])).then_inc(S["bsel_ok"], 1)
            step(nc.gpsimd.tensor_copy(pay[:, :, 3 * D], token1))

            def gate_rows(k):
                gp.wait_ge(S["mod_bc_copied"], 2 * BC * (k + 1))
                for b in range(BC * k, BC * (k + 1)):
                    nc.gpsimd.tensor_copy(pay[:, 2 * b:2 * b + 2, 2 * D:3 * D],
                                          mod_b[:, b, 5 * D:6 * D].unsqueeze(1).to_broadcast([P, 2, D])
                                          ).then_inc(S["gate_rows"], 1)

            def inverse_root(which, src, eps, ready, done, k):
                gp.wait_ge(ready, k + 1)
                step(nc.gpsimd.tensor_scalar(rs[:, which, :], src, eps, None, ALU.add))
                settle()
                nc.gpsimd.tensor_tensor(rs[:, which, :], rs[:, which, :], half, ALU.pow).then_inc(done, 1)

            def ln_rstd(k):
                inverse_root(0, mv[:, 0, :, 1], 1e-5, S["ln_var"], S["ln_rstd"], k)

            def rms_rs(k):
                inverse_root(1, ss[:, 0, :], 1e-6, S["rms_ss"], S["rms_rs"], k)

            def rms2_rs(k):
                inverse_root(2, ss[:, 1, :], 1e-6, S["rms2_ss"], S["rms2_rs"], k)

            def ln2_rstd(k):
                inverse_root(3, mv[:, 1, :, 1], 1e-5, S["ln2_var"], S["ln2_rstd"], k)

            def step_size(k):
                if k == 0:
                    return
                b = k % 2
                gp.wait_ge(S["dp_ln"], k + 1)
                gp.wait_ge(S["dp_max"], NH * (k + 1))
                nc.gpsimd.tensor_tensor(delta[:, b], delta[:, b], soft, ALU.add).then_inc(S["delta_ok"], 1)

            def step_input(k):
                if k == 0:
                    return
                b = k % 2
                gp.wait_ge(S["delta_ok"], k + 1)
                gp.wait_ge(S["u_ok"], NH * (k + 1))
                nc.gpsimd.tensor_tensor(du[:, b], delta[:, b], u[:, b], ALU.mult).then_inc(S["du_ok"], 1)

            def gate_y(k):
                if k == NC - 1:
                    return
                gp.wait_ge(S["y_read"], k + 1)
                nc.gpsimd.tensor_tensor(u[:, k % 2], u[:, k % 2], zg[:, k % 2], ALU.mult).then_inc(S["yg_ok"], 1)

            def stay(k):
                gp.wait_ge(S["hm_ok"], k + 1)
                gp.wait_ge(S["gate_rows"], BC * (k + 1))
                if k:
                    gp.wait_ge(S["base_out"], 16 * k)
                t = pay[:, chunk(k), :]
                step(nc.gpsimd.tensor_tensor(base[:], t[:, :, 0:D], t[:, :, 2 * D:3 * D], ALU.mult))
                settle()
                nc.gpsimd.tensor_tensor(base[:], base[:], t[:, :, D:2 * D], ALU.add).then_inc(S["base_ok"], 1)

            def drive_step(k):
                c, n = divmod(k, STEPS)
                if n == 0:
                    gp.wait_ge(S["du_ok"], c + 1)
                gp.wait_ge(S["b_copied"], k + 1)
                if k >= 2:
                    gp.wait_ge(S["scanned"], NH * (k - 1))
                nc.gpsimd.tensor_tensor(
                    drive[:, n % 2, :].rearrange("p (h t) -> p h t", h=NH), du[:, c % 2],
                    b_rows[:, n % 4, :].unsqueeze(1).to_broadcast([P, NH, CH]), ALU.mult).then_inc(S["drive_ok"], 1)

            beside = BESIDE(("GB_P", gate_rows), ("LN_P", ln_rstd), ("RMS_P", rms_rs), ("DELTA_P", step_size), ("DU_P", step_input),
                            ("GATE_P", gate_y), ("RMS2_P", rms2_rs), ("LN2_P", ln2_rstd), ("STAY_P", stay))
            beside(-99, -1)
            for k in range(NC * STEPS):
                drive_step(k)
                beside(k, k)
            beside(NC * STEPS, 999)

            gp.wait_ge(S["dram_zeroed"], 16 * (ST // 4))
            for g, (i, j) in enumerate(GROUPS):
                gp.wait_ge(S["compared"], last_unit(j - 1))
                gp.wait_ge(S["rank_ok"], 1 + (j > EARLY))
                r, s = rank[:, i:j], slot_f[:, :, i:j]
                step(nc.gpsimd.tensor_tensor(r, r, cnt[:, COUNTS - 1, i:j], ALU.add))
                settle()
                step(nc.gpsimd.tensor_scalar(s[:, 0, :], r, float(CAP), FAR, ALU.is_ge, ALU.mult))
                step(nc.gpsimd.tensor_tensor(s[:, 1, :], r, first[:, i:j], ALU.add))
                settle()
                step(nc.gpsimd.tensor_tensor(s[:, 0, :], s[:, 0, :], s[:, 1, :], ALU.add))
                settle()
                nc.gpsimd.tensor_copy(slot[:, i:j], s[:, 0, :]).then_inc(S["slot_ok"], 1)
                gp.wait_ge(S["slot_ok"], g + 1)
                for t in range(i, j):
                    nc.gpsimd.indirect_dma_start(
                        xe_dram, bass.IndirectOffsetOnAxis(ap=slot[:, t:t + 1], axis=0), pay[:, t, :], None,
                        bounds_check=SLOTS - 1, oob_is_err=False).then_inc(S["rows_out"], 16)

            gp.wait_ge(S["xe_rest"], 16 * (ST // 4))
            step(nc.gpsimd.tensor_scalar(tok_f[:, :, 0], xe[:, :, 3 * D], 0.0, FAR, ALU.is_equal, ALU.mult))
            step(nc.gpsimd.tensor_scalar(tok_f[:, :, 1], xe[:, :, 3 * D], -1.0, None, ALU.add))
            settle()
            step(nc.gpsimd.tensor_tensor(tok_f[:, :, 0], tok_f[:, :, 0], tok_f[:, :, 1], ALU.add))
            settle()
            step(nc.gpsimd.tensor_copy(tok[:], tok_f[:, :, 0]))
            settle()
            gp.wait_ge(S["base_out"], 16 * NC)
            flat = out.rearrange("b t d -> (b t) d")
            for s in range(ST):
                gp.wait_ge(S["fin_ok"], 1 + sum(b <= s for a, b in OUT))
                nc.gpsimd.indirect_dma_start(
                    flat, bass.IndirectOffsetOnAxis(ap=tok[:, s:s + 1], axis=0), fin[:, s, :], None,
                    bounds_check=TOK - 1, oob_is_err=False).then_inc(S["final_out"], 16)

        @block.scalar
        def _(act):
            act.wait_ge(S["ld_mod"], 32)
            nc.scalar.activation(silu_c[:], c_t[:], ACT.Silu).then_inc(S["silu_c_ok"], 1)
            act.wait_ge(S["mod_mm"], 2)
            nc.scalar.activation(mod[:, 0:CH], side[0][0:PARTS * NB, :], ACT.Copy).then_inc(S["mod_raw"], 1)
            nc.scalar.activation(mod[:, CH:6 * D], side[1][0:PARTS * NB, 0:6 * D - CH], ACT.Copy).then_inc(S["mod_raw"], 1)
            act.wait_ge(S["ld_w"], 16 * 5)
            nc.scalar.activation(neg_a[:], chan[:, :, TAPS + 3:], ACT.Exp).then_inc(S["act_step"], 1)

            def copy_modulation(first):
                for b in range(first, first + 2):
                    lo, hi = ps[:, 4 * (b % 2), :], ps[:, 4 * (b % 2) + 1, 0:6 * D - CH]
                    act.wait_ge(S["mod_bc"], 2 * b + 2)
                    nc.scalar.activation(mod_b[:, b, 0:CH], lo, ACT.Copy).then_inc(S["mod_bc_copied"], 1)
                    nc.scalar.activation(mod_b[:, b, CH:6 * D], hi, ACT.Copy).then_inc(S["mod_bc_copied"], 1)

            def more_modulation(k):
                if k < NC - 1:
                    copy_modulation(BC * (k + 1))

            copy_modulation(0)

            def square_sums(which, ready, used, done):
                def stage(k):
                    act.wait_ge(S[ready], k + 1)
                    if k:
                        act.wait_ge(S[used], k)
                    for t in range(TC):
                        ins = nc.scalar.activation(hn[:, which, t, :], h[:, k % 4, t, :], ACT.Square,
                                                   accum_out=ss[:, which, t:t + 1])
                    ins.then_inc(S[done], 1)
                return stage

            def scaled(which, rstd, done):
                def stage(k):
                    act.wait_ge(S[rstd], k + 1)
                    for t in range(TC):
                        ins = nc.scalar.activation(hn[:, which, t, :], h[:, k % 4, t, :], ACT.Copy,
                                                   scale=rs[:, 1 + which, t:t + 1])
                    ins.then_inc(S[done], 1)
                return stage

            def to_h_t(k):
                act.wait_ge(S["hn_tr"], k + 1)
                if k:
                    act.wait_ge(S["z_mm"], NH * k)
                nc.scalar.activation(h_t[:, 0, :], side[0], ACT.Copy, scale=cols[:, 0:1]).then_inc(S["h_t_ok"], 1)

            def last_tap(j):
                def stage(k):
                    if k >= 2:
                        act.wait_ge(S["op_mm"], 2 * (k - 1))
                    act.wait_ge(S["xm_mm"], NH * k + j + 1)
                    nc.scalar.activation(u[:, k % 2, j, :], side[j], ACT.Identity, bias=chan[:, j, TAPS:TAPS + 1],
                                         scale=chan[:, j, TAPS - 1:TAPS]).then_inc(S["conv0"], 1)
                return stage

            def silu_u(j):
                def stage(k):
                    act.wait_ge(S["conv_ok"], NH * k + j + 1)
                    nc.scalar.activation(u[:, k % 2, j, :], u[:, k % 2, j, :], ACT.Silu).then_inc(S["u_ok"], 1)
                return stage

            def silu_z(j):
                def stage(k):
                    if k >= 2:
                        act.wait_ge(S["yg_ok"], k - 1)
                    act.wait_ge(S["z_mm"], NH * k + j + 1)
                    nc.scalar.activation(zg[:, k % 2, j, :], side[j], ACT.Silu).then_inc(S["z_ok"], 1)
                return stage

            def first_part(k):
                act.wait_ge(S["dbc_mm"], k + 1)
                if k:
                    act.wait_ge(S["dbc_ok"], k)
                    act.wait_ge(S["dp_mm"], NH * k)
                nc.scalar.activation(dbc_hi[:], side[0][0:PARTS * G, :], ACT.Copy).then_inc(S["dbc_copied"], 1)
                nc.scalar.activation(dt_rows[:], side[0][0:RANK, :], ACT.Copy).then_inc(S["dt_ok"], 1)

            def second_part(k):
                act.wait_ge(S["dbc_r1"], k + 1)
                nc.scalar.activation(dbc_hi[:], dbc_t[:], ACT.Copy).then_inc(S["dbc_mid"], 1)

            def step_abs(j):
                def stage(k):
                    if k:
                        act.wait_ge(S["delta_ok"], k)
                    act.wait_ge(S["dp_max"], NH * k + j + 1)
                    nc.scalar.activation(soft[:, j, :], side[j], ACT.Abs, bias=chan[:, j, TAPS + 1:TAPS + 2]
                                         ).then_inc(S["dp_abs"], 1)
                return stage

            def softplus(k):
                act.wait_ge(S["dp_abs"], NH * (k + 1))
                nc.scalar.activation(soft, soft, ACT.Exp, scale=-1.0).then_inc(S["dp_exp"], 1)
                act.wait_ge(S["dp_exp"], k + 1)
                nc.scalar.activation(soft, soft, ACT.Ln, bias=1.0).then_inc(S["dp_ln"], 1)

            def to_h2_t(k):
                act.wait_ge(S["hn2_tr"], k + 1)
                if k:
                    act.wait_ge(S["f1_mm"], FB * k)
                nc.scalar.activation(h_t[:, 1, :], side[1], ACT.Copy, scale=cols[:, 1:2]).then_inc(S["h2_t_ok"], 1)

            def gelu(f):
                def stage(k):
                    if f == 0:
                        if k == 0:
                            act.wait_ge(S["dram_zeroed"], 16 * (ST // 4))
                        else:
                            act.wait_ge(S["f2_mm"], 2 * k)
                    act.wait_ge(S["f1_mm"], FB * k + f + 1)
                    nc.scalar.activation(m_t[:, f, :], side[1 - f % 2], ACT.Gelu, bias=cols[:, 2 + f:3 + f]
                                         ).then_inc(S["gelu_ok"], 1)
                return stage

            def to_hm_t(k):
                act.wait_ge(S["hm_tr"], k + 1)
                if k:
                    act.wait_ge(S["lg_mm"], k)
                nc.scalar.activation(h_t[:, 2, :], side[1], ACT.Copy).then_inc(S["hm_t_ok"], 1)

            def copy_b(k):
                act.wait_ge(S["b_bcast"], k + 1)
                if k >= 4:
                    act.wait_ge(S["drive_ok"], k - 3)
                nc.scalar.activation(b_rows[:, k % 4, :], bank_b, ACT.Copy).then_inc(S["b_copied"], 1)

            def decay_step(k):
                c, n = divmod(k, STEPS)
                if n == 0:
                    act.wait_ge(S["delta_ok"], c + 1)
                for j in range(NH):
                    if k:
                        act.wait_ge(S["scanned"], NH * (k - 1) + j + 1)
                    nc.scalar.activation(decay[:, j, :].rearrange("p (b t) -> p b t", b=BC)[:, :, 1:T],
                                         delta[:, c % 2, j, :].rearrange("p (b t) -> p b t", b=BC)[:, :, 1:T], ACT.Exp,
                                         scale=neg_a[:, j, n:n + 1]).then_inc(S["decay_ok"], 1)

            def exponentials(a, b):
                act.wait_ge(S["e_d"], 1 + (a > 0))
                nc.scalar.activation(msk[:, a:b, :], sm[:, a:b, :], ACT.Exp).then_inc(S["e_exp"], 1)

            def to_expert_rows(a, b):
                if a == 0:
                    act.wait_ge(S["op_mm"], 2 * (NC - 1))
                act.wait_ge(S["rt_tr"], 2 * b)
                rows = expert_rows(1, a)[:, 0:(b - a) * P]
                nc.scalar.activation(h_rows[:, a * P:b * P], rows, ACT.Copy).then_inc(S["h_rows_ok"], 1)
                act.wait_ge(S["ln2_var"], b // TC)
                act.wait_ge(S["h_rows_ok"], 1 + (a > 0))
                nc.scalar.activation(hot_t[:, a * P:b * P], h_rows[0:NE, a * P:b * P], ACT.Copy).then_inc(S["hot_t_ok"], 1)

            beside = BESIDE(("R_EXP_A", lambda k: exponentials(0, EARLY)), ("R_ROWS_A", lambda k: to_expert_rows(0, EARLY)),
                            ("R_EXP2_A", lambda k: exponentials(EARLY, NT)), ("R_ROWS2_A", lambda k: to_expert_rows(EARLY, NT)),
                            ("SQ_A", square_sums(0, "h_ok", "hn_tr", "rms_ss")), ("RMSA_A", scaled(0, "rms_rs", "hn_ok")),
                            ("SQ2_A", square_sums(1, "h2_ok", "hn2_tr", "rms2_ss")),
                            ("RMS2A_A", scaled(1, "rms2_rs", "hn2_ok")), ("MB_A", more_modulation), ("HT_A", to_h_t), ("TAP0_A", last_tap(0)), ("TAP1_A", last_tap(1)),
                            ("SILU0_A", silu_u(0)), ("SILU1_A", silu_u(1)), ("SZ0_A", silu_z(0)), ("SZ1_A", silu_z(1)),
                            ("PART1_A", first_part), ("PART2_A", second_part), ("ABS0_A", step_abs(0)),
                            ("ABS1_A", step_abs(1)), ("SOFT_A", softplus), ("H2T_A", to_h2_t), ("GELU0_A", gelu(0)),
                            ("GELU1_A", gelu(1)), ("GELU2_A", gelu(2)), ("GELU3_A", gelu(3)), ("HMT_A", to_hm_t))
            beside(-99, -1)
            act.wait_ge(S["neg_a_ok"], 1)
            act.wait_ge(S["decay_zeroed"], 1)
            for k in range(B_COPIED):
                copy_b(k)
            for k in range(NC * STEPS):
                decay_step(k)
                if k + B_COPIED < NC * STEPS:
                    copy_b(k + B_COPIED)
                beside(k, k)
            beside(NC * STEPS, 999)

            for e in range(NE):
                act.wait_ge(S["e1_mm"], e + 1)
                if e >= 2:
                    act.wait_ge(S["e2_mm"], e - 1)
                for j in range(2):
                    nc.scalar.activation(g_t[:, e % 2, j, :], ps[:, 2 + e % 2, j * CAP:(j + 1) * CAP], ACT.Gelu_apprx_tanh,
                                         bias=cols[:, 2 + FB + 2 * e + j:3 + FB + 2 * e + j]).then_inc(S["e1_ok"], 1)

        @block.vector
        def _(dve):
            n_step = [0]

            def step(ins):
                n_step[0] += 1
                ins.then_inc(S["dve_step"], 1)

            def settle():
                dve.wait_ge(S["dve_step"], n_step[0])

            v = nc.vector
            step(v.memset(minus16[:, 1:2], 1.0))
            step(v.memset(minus16[:, 0:1], -1.0))
            v.memset(decay.rearrange("p h (b t) -> p (h b) t", t=T)[:, :, 0:1], 0.0).then_inc(S["decay_zeroed"], 1)

            def modulation():
                dve.wait_ge(S["mod_raw"], 2)
                m6 = mod.rearrange("p (k s d) -> p k s d", k=2, s=3)
                t6 = mod_t.rearrange("p (k s d) -> p k s d", k=2, s=3)
                step(v.tensor_scalar(m6[:, :, 1, :], m6[:, :, 1, :], 1.0, None, ALU.add))
                step(v.tensor_scalar(t6[:, :, 0, :], m6[:, :, 2, :], 0.0, 2.0, ALU.is_ge, ALU.mult))
                step(v.scalar_tensor_tensor(t6[:, :, 1, :], m6[:, :, 2, :], -1.0, m6[:, :, 2, :], ALU.mult, ALU.max))
                settle()
                step(v.tensor_scalar(t6[:, :, 1, :], t6[:, :, 1, :], 0.25, None, ALU.max))
                settle()
                step(v.scalar_tensor_tensor(m6[:, :, 2, :], t6[:, :, 0, :], -1.0, t6[:, :, 1, :], ALU.add, ALU.mult))
                settle()
                step(v.tensor_copy(mod_hi, mod))
                settle()
                step(v.scalar_tensor_tensor(mod_t, mod_hi, cut_m[:, 0:1], mod, ALU.mult, ALU.add))
                settle()
                step(v.tensor_copy(mod_hi, mod_t))
                settle()
                v.scalar_tensor_tensor(mod_parts, mod_hi, cut_m[:, 1:2], mod_t, ALU.mult, ALU.add
                                       ).then_inc(S["mod_parts_ok"], 1)

            def rows_of(c, section):
                r = mod_b[:, BC * c:BC * (c + 1), section * D:(section + 1) * D]
                return r.unsqueeze(2).to_broadcast([P, BC, TC // BC, D])

            def by_batch(t):
                return t.rearrange("p (b k) d -> p b k d", b=BC)

            def statistics(which, src, ready):
                for t in range(TC):
                    step(v.bn_stats(bn[:, which, t, :], src[:, t, :]))
                settle()
                for t in range(TC):
                    ins = v.bn_aggr(mv[:, which, t, :], bn[:, which, t, :])
                    if t < TC - 1:
                        step(ins)
                ins.then_inc(ready, 1)

            def standardise(which, src, dst):
                for t in range(TC):
                    step(v.tensor_scalar(dst[:, t, :], src[:, t, :], mv[:, which, t, 0:1],
                                         rs[:, 3 * which, t:t + 1], ALU.subtract, ALU.mult))
                settle()

            def ln_stats(k):
                dve.wait_ge(S["ld_x"][k], 16)
                statistics(0, x[:, chunk(k), :], S["ln_var"])

            def ln_apply(k):
                hk = h[:, k % 4]
                dve.wait_ge(S["mod_bc_copied"], 2 * BC * (k + 1))
                dve.wait_ge(S["ln_var"], k + 1)
                dve.wait_ge(S["ln_rstd"], k + 1)
                standardise(0, x[:, chunk(k), :], hk)
                step(v.tensor_tensor(by_batch(hk), by_batch(hk), rows_of(k, CA), ALU.mult))
                settle()
                v.tensor_tensor(by_batch(hk), by_batch(hk), rows_of(k, SA), ALU.add).then_inc(S["h_ok"], 1)

            def other_taps(j):
                def stage(k):
                    dve.wait_ge(S["conv0"], NH * k + j + 1)
                    xm = side[j].rearrange("p (b t) -> p b t", b=BC)
                    acc = u[:, k % 2, j, :].rearrange("p (b t) -> p b t", b=BC)
                    for s in range(1, TAPS):
                        ins = v.scalar_tensor_tensor(acc[:, :, s:T], xm[:, :, 0:T - s],
                                                     chan[:, j, TAPS - 1 - s:TAPS - s], acc[:, :, s:T], ALU.mult, ALU.add)
                        if s < TAPS - 1:
                            step(ins)
                            settle()
                    ins.then_inc(S["conv_ok"], 1)
                return stage

            def first_rest(k):
                dve.wait_ge(S["dbc_copied"], k + 1)
                dve.wait_ge(S["dt_ok"], k + 1)
                v.scalar_tensor_tensor(dbc_t[:], dbc_hi[:], cut_g[:, 0:1], side[0][0:PARTS * G, :], ALU.mult, ALU.add
                                       ).then_inc(S["dbc_r1"], 1)

            def parts_of(k):
                dve.wait_ge(S["dbc_mid"], k + 1)
                v.scalar_tensor_tensor(dbc_parts[:, k % 2, :], dbc_hi[:], cut_g[:, 1:2], dbc_t[:], ALU.mult, ALU.add
                                       ).then_inc(S["dbc_ok"], 1)

            def positive_part(j):
                def stage(k):
                    dve.wait_ge(S["dp_mm"], NH * k + j + 1)
                    v.tensor_scalar(delta[:, k % 2, j, :], side[j], chan[:, j, TAPS + 1:TAPS + 2], 0.0, ALU.add, ALU.max
                                    ).then_inc(S["dp_max"], 1)
                return stage

            def y_out(k):
                dve.wait_ge(S["summed"], STEPS * (k + 1))
                dve.wait_ge(S["z_ok"], NH * (k + 1))
                for j in range(NH):
                    ins = v.scalar_tensor_tensor(u[:, k % 2, j, :], u[:, k % 2, j, :], chan[:, j, TAPS + 2:TAPS + 3],
                                                 ysum[:, j, :], ALU.mult, ALU.add)
                    if j < NH - 1:
                        step(ins)
                ins.then_inc(S["y_read"], 1)
                if k == NC - 1:
                    dve.wait_ge(S["y_read"], NC)
                    v.tensor_tensor(u[:, k % 2], u[:, k % 2], zg[:, k % 2], ALU.mult).then_inc(S["yg_ok"], 1)

            def residual(k):
                hk = h[:, k % 4]
                dve.wait_ge(S["op_mm"], 2 * (k + 1))
                v.tensor_tensor(hk, side[0].rearrange("p (t d) -> p t d", d=D), hk, ALU.add).then_inc(S["h2_ok"], 1)

            def stream(k):
                hk = h[:, k % 4]
                dve.wait_ge(S["f2_mm"], 2 * (k + 1))
                v.tensor_tensor(hk, side[1].rearrange("p (t d) -> p t d", d=D), hk, ALU.add).then_inc(S["f2_read"], 1)
                dve.wait_ge(S["f2_read"], k + 1)
                step(v.tensor_tensor(by_batch(hk), by_batch(hk), rows_of(k, GA), ALU.mult))
                settle()
                x1 = pay[:, chunk(k), D:2 * D]
                step(v.tensor_tensor(x1, hk, x[:, chunk(k), :], ALU.add))
                settle()
                statistics(1, x1, S["ln2_var"])

            def ln2_apply(k):
                hm = pay[:, chunk(k), 0:D]
                dve.wait_ge(S["ln2_var"], k + 1)
                dve.wait_ge(S["ln2_rstd"], k + 1)
                standardise(1, pay[:, chunk(k), D:2 * D], hm)
                step(v.tensor_tensor(by_batch(hm), by_batch(hm), rows_of(k, CB), ALU.mult))
                settle()
                v.tensor_tensor(by_batch(hm), by_batch(hm), rows_of(k, SB), ALU.add).then_inc(S["hm_ok"], 1)

            def keep_logits(k):
                dve.wait_ge(S["lg_mm"], k + 1)
                v.tensor_copy(logits[:, chunk(k), :], side[1][:, 0:TC * NE].rearrange("p (t e) -> p t e", e=NE)
                              ).then_inc(S["lg_ok"], 1)

            def scan_step(k):
                dve.wait_ge(S["drive_ok"], k + 1)
                if k >= 4:
                    dve.wait_ge(S["weighted"], k - 3)
                for j in range(NH):
                    dve.wait_ge(S["decay_ok"], NH * k + j + 1)
                    v.tensor_tensor_scan(state[:, k % 4, j * CH:(j + 1) * CH], decay[:, j, :],
                                         drive[:, k % 2, j * CH:(j + 1) * CH], 0.0, ALU.mult, ALU.add
                                         ).then_inc(S["scanned"], 1)

            def weight_step(k):
                dve.wait_ge(S["c_bcast"], k + 1)
                dve.wait_ge(S["scanned"], NH * (k + 1))
                if k >= 2:
                    dve.wait_ge(S["summed"], k - 1)
                v.tensor_tensor(part[:, k % 2, :].rearrange("p (h t) -> p h t", h=NH),
                                state[:, k % 4, :].rearrange("p (h t) -> p h t", h=NH),
                                bank_c.unsqueeze(1).to_broadcast([P, NH, CH]), ALU.mult).then_inc(S["weighted"], 1)

            def choose(a, b):
                def per_token(t):
                    return t[:, a:b].unsqueeze(2).to_broadcast([P, b - a, NE])

                dve.wait_ge(S["lg_ok"], b // TC)
                step(v.tensor_reduce(top[:, a:b], logits[:, a:b, :], AX_X, ALU.max))
                settle()
                v.tensor_tensor(sm[:, a:b, :], logits[:, a:b, :], per_token(top), ALU.subtract).then_inc(S["e_d"], 1)
                dve.wait_ge(S["e_d"], 1 + (a > 0))
                choice = hot[:, a:b, :]
                step(v.tensor_scalar(choice, sm[:, a:b, :], 0.0, None, ALU.is_equal))
                settle()
                step(v.tensor_tensor(choice, choice, prefer.unsqueeze(1).to_broadcast([P, b - a, NE]), ALU.mult))
                settle()
                step(v.tensor_reduce(first[:, a:b], choice, AX_X, ALU.max))
                settle()
                step(v.tensor_tensor(choice, choice, per_token(first), ALU.is_equal))
                settle()
                step(v.tensor_scalar(first[:, a:b], first[:, a:b], -float(CAP), float(CAP * NE), ALU.mult, ALU.add))

            def split(a, b):
                values, choice = msk[:, a:b, :], hot[:, a:b, :]
                dve.wait_ge(S["e_exp"], 1 + (a > 0))
                step(v.tensor_reduce(top[:, a:b], values, AX_X, ALU.add))
                settle()
                step(v.reciprocal(top[:, a:b], top[:, a:b]))
                settle()
                step(v.tensor_tensor(values, choice, top[:, a:b].unsqueeze(2).to_broadcast([P, b - a, NE]), ALU.mult))
                settle()
                step(v.scalar_tensor_tensor(values, choice, -1.0, values, ALU.add, ALU.add))
                settle()
                for k in range(PARTS):
                    step(v.tensor_copy(h_parts[:, a:b, k, :], choice))
                    step(v.tensor_copy(m_parts[:, a:b, k, :], values))
                    settle()
                    if k < PARTS - 1:
                        step(v.tensor_tensor(values, values, m_parts[:, a:b, k, :], ALU.subtract))
                        settle()
                v.memset(cnt[:, :, a:b], 0.0).then_inc(S["parts_ok"], 1)
                dve.wait_ge(S["parts_ok"], 1 + (a > 0))

            def value_rows(a, b):
                if a == 0:
                    dve.wait_ge(S["yg_ok"], NC - 1)
                dve.wait_ge(S["rt_tr"], 2 * a + (b - a))
                rows = expert_rows(0, a)[:, 0:(b - a) * P]
                v.tensor_copy(m_rows[:, a * P:b * P], rows).then_inc(S["m_rows_ok"], 1)

            def compare(q):
                t, i, j = units[q]
                mine = top[:, t:t + 1]
                dve.wait_ge(S["row_mm"], q + 1)
                row = unit_bank(q, (j - i) * P)
                if i == t:
                    if t >= 2:
                        dve.wait_ge(S["compared"], q - 1)
                    step(v.scalar_tensor_tensor(equal[:, t % 2, :], row[:, 0:P], mine, earlier, ALU.is_equal, ALU.mult,
                                                accum_out=cnt[:, 0, t:t + 1]))
                n = COUNTS - 1 if q >= len(unit_a) else 1 + (i - t) // TC
                v.tensor_scalar(greater[t][:, (i - t) * P:(j - t) * P], row, mine, None, ALU.is_gt, ALU.add,
                                accum_out=cnt[:, n, t:t + 1]).then_inc(S["compared"], 1)

            def early_choice(k):
                step(v.tensor_copy(id16[:], ident))
                step(v.memset(ones_e[:], 1.0))
                step(v.memset(tiles_before[:, :, 0:1], 0.0))
                choose(0, EARLY)

            def early_split(k):
                split(0, EARLY)

            def earlier_tiles(which, bank, n):
                dve.wait_ge(S["counts_mm"], which + 1)
                v.tensor_tensor_scan(tiles_before[:, which, 1:n], ones_e[:, 1:n], ps[0:NE, bank, 0:n - 1], 0.0,
                                     ALU.mult, ALU.add).then_inc(S["prefix_ok"], 1)

            def early_values(k):
                value_rows(0, EARLY)
                earlier_tiles(0, 4, EARLY)

            def last_choice(k):
                choose(EARLY, NT)

            def last_split(k):
                split(EARLY, NT)

            def last_values(k):
                value_rows(EARLY, NT)

            def early_compare(k):
                for q, (t, i, j) in enumerate(unit_a):
                    if t // (EARLY // 4) == k:
                        compare(q)

            beside = BESIDE(("R_CHOOSE_V", early_choice), ("R_SPLIT_V", early_split), ("R_VALUES_V", early_values),
                            ("R_CMP_V", early_compare), ("R_CHOOSE2_V", last_choice),
                            ("R_SPLIT2_V", last_split), ("R_VALUES2_V", last_values), ("LN_V", ln_stats), ("LNA_V", ln_apply), ("TAP0_V", other_taps(0)),
                            ("TAP1_V", other_taps(1)), ("REST_V", first_rest), ("PARTS_V", parts_of),
                            ("POS0_V", positive_part(0)), ("POS1_V", positive_part(1)), ("Y_V", y_out),
                            ("RES_V", residual), ("STREAM_V", stream), ("LN2A_V", ln2_apply),
                            ("LG_V", keep_logits))
            beside(-99, -99)
            modulation()
            dve.wait_ge(S["act_step"], 1)
            v.tensor_scalar(neg_a[:], neg_a[:], -1.0, None, ALU.mult).then_inc(S["neg_a_ok"], 1)
            dve.wait_ge(S["ld_const"], 16)
            v.tensor_copy(sel[:], sel_rows.unsqueeze(2).to_broadcast([PARTS * G, 2 * NS, P])).then_inc(S["sel_ok"], 1)
            beside(-98, -1)
            dve.wait_ge(S["dp_ln"], 1)
            v.tensor_tensor(delta[:, 0], delta[:, 0], soft, ALU.add).then_inc(S["delta_ok"], 1)
            dve.wait_ge(S["delta_ok"], 1)
            v.tensor_tensor(du[:, 0], delta[:, 0], u[:, 0], ALU.mult).then_inc(S["du_ok"], 1)
            scan_step(0)
            for k in range(NC * STEPS):
                if k + 1 < NC * STEPS:
                    scan_step(k + 1)
                weight_step(k)
                beside(k, k)
            beside(NC * STEPS, 999)

            earlier_tiles(1, 7, NT)
            dve.wait_ge(S["compared"], len(unit_a))
            step(v.tensor_reduce(counted[:], cnt[:, 0:COUNTS - 1, 0:EARLY].rearrange("p n t -> p t n"), AX_X, ALU.add))
            settle()
            dve.wait_ge(S["before_mm"], EARLY)
            v.tensor_tensor(rank[:, 0:EARLY], ps[:, 4, 0:EARLY], counted[:], ALU.add).then_inc(S["rank_ok"], 1)
            for q in range(len(unit_a), len(units)):
                compare(q)
            dve.wait_ge(S["before_mm"], NT)
            dve.wait_ge(S["compared"], len(units))
            v.tensor_tensor(rank[:, EARLY:NT], ps[:, 7, EARLY:NT], cnt[:, 0, EARLY:NT], ALU.add).then_inc(S["rank_ok"], 1)

            for s in range(0, ST, 4):
                g = s // 4
                dve.wait_ge(S["xt_tr"], g + 1)
                v.tensor_copy(xe_t[:, s * P:(s + 4) * P], ps[:, g % 2, :]).then_inc(S["xt_ok"], 1)
            def put_out(g):
                a, b = OUT[g]
                dve.wait_ge(S["o_tr"], g + 1)
                if g == 0:
                    dve.wait_ge(S["xe_rest"], 16 * (ST // 4))
                f = fin[:, a:b, :]
                step(v.tensor_tensor(f, ps[:, 6 + g % 2, 0:(b - a) * P].rearrange("p (s d) -> p s d", d=D),
                                     xe[:, a:b, 2 * D:3 * D], ALU.mult))
                settle()
                v.tensor_tensor(f, f, xe[:, a:b, D:2 * D], ALU.add).then_inc(S["fin_ok"], 1)

            g = 0
            for e in range(NE):
                dve.wait_ge(S["e2_mm"], e + 1)
                v.tensor_scalar(o_t[:, e * CAP:(e + 1) * CAP], ps[:, 4 + e % 2, 0:CAP],
                                cols[:, 2 + FB + 2 * NE + e:3 + FB + 2 * NE + e], None, ALU.add).then_inc(S["e2_ok"], 1)
                while OUT[g][1] * P <= e * CAP:
                    put_out(g)
                    g += 1
            while g < len(OUT):
                put_out(g)
                g += 1

        @block.tensor
        def _(pe):
            mm = nc.tensor.matmul
            pe.wait_ge(S["silu_c_ok"], 1)
            mm(side[0][0:PARTS * NB, :], silu_c[:], w_mod[:, 0:CH], start=True, stop=True).then_inc(S["mod_mm"], 1)
            mm(side[1][0:PARTS * NB, 0:6 * D - CH], silu_c[:], w_mod[:, CH:6 * D], start=True, stop=True
               ).then_inc(S["mod_mm"], 1)
            pe.wait_ge(S["mod_parts_ok"], 1)
            pe.wait_ge(S["bsel_ok"], 1)

            def broadcast_modulation(first):
                for b in range(first, first + 2):
                    if b >= 2:
                        pe.wait_ge(S["mod_bc_copied"], 2 * (b - 1))
                    mm(ps[:, 4 * (b % 2), :], bsel[:, b, :], mod_parts[:, 0:CH], start=True, stop=True
                       ).then_inc(S["mod_bc"], 1)
                    mm(ps[:, 4 * (b % 2) + 1, 0:6 * D - CH], bsel[:, b, :], mod_parts[:, CH:6 * D], start=True, stop=True
                       ).then_inc(S["mod_bc"], 1)

            def more_modulation(k):
                if k < NC - 1:
                    broadcast_modulation(BC * (k + 1))

            broadcast_modulation(0)

            def to_channels(bank, src, done):
                for t in range(TC):
                    ins = nc.tensor.transpose(bank[:, t * P:(t + 1) * P], src[:, t, :], ident)
                ins.then_inc(done, 1)

            reader = [(S["mod_raw"], 2)] * 2

            def take_side(b, read, count):
                pe.wait_ge(*reader[b])
                reader[b] = (S[read], count)
                return side[b]

            def hn_to_channels(k):
                pe.wait_ge(S["hn_ok"], k + 1)
                to_channels(take_side(0, "h_t_ok", k + 1), hn[:, 0], S["hn_tr"])

            def in_proj_x(j):
                def stage(k):
                    pe.wait_ge(S["h_t_ok"], k + 1)
                    if k == 0:
                        pe.wait_ge(S["ld_w"], 16 * 5)
                    mm(take_side(j, "conv_ok", NH * k + j + 1), w_in[:, j * P:(j + 1) * P], h_t[:, 0, :],
                       start=True, stop=True).then_inc(S["xm_mm"], 1)
                return stage

            def in_proj_z(j):
                def stage(k):
                    mm(take_side(j, "z_ok", NH * k + j + 1), w_in[:, DI + j * P:DI + (j + 1) * P], h_t[:, 0, :],
                       start=True, stop=True).then_inc(S["z_mm"], 1)
                return stage

            def x_proj(k):
                pe.wait_ge(S["u_ok"], NH * (k + 1))
                bank = take_side(0, "dbc_r1", k + 1)
                for j in range(NH):
                    ins = mm(bank[0:PARTS * G, :], w_xp[:, j, :], u[:, k % 2, j, :], start=(j == 0), stop=(j == NH - 1))
                ins.then_inc(S["dbc_mm"], 1)

            def dt_proj(j):
                def stage(k):
                    pe.wait_ge(S["dt_ok"], k + 1)
                    mm(take_side(j, "dp_abs", NH * k + j + 1), w_dt[:, j * P:(j + 1) * P], dt_rows[:],
                       start=True, stop=True).then_inc(S["dp_mm"], 1)
                return stage

            def out_proj(part):
                def stage(k):
                    if part == 0:
                        if k == 0:
                            pe.wait_ge(S["ld_m"], 16 * 5)
                        pe.wait_ge(S["yg_ok"], k + 1)
                        take_side(0, "h2_ok", k + 1)
                    for t in range(2 * part, 2 * part + 2):
                        for j in range(NH):
                            ins = mm(side[0][:, t * D:(t + 1) * D], u[:, k % 2, j, t * P:(t + 1) * P], w_out[:, j, :],
                                     start=(j == 0), stop=(j == NH - 1))
                    ins.then_inc(S["op_mm"], 1)
                return stage

            def hn2_to_channels(k):
                pe.wait_ge(S["hn2_ok"], k + 1)
                to_channels(take_side(1, "h2_t_ok", k + 1), hn[:, 1], S["hn2_tr"])

            def mlp_up(f):
                def stage(k):
                    pe.wait_ge(S["h2_t_ok"], k + 1)
                    mm(take_side(1 - f % 2, "gelu_ok", FB * k + f + 1), w_m1[:, f * P:(f + 1) * P], h_t[:, 1, :],
                       start=True, stop=True).then_inc(S["f1_mm"], 1)
                return stage

            def mlp_down(part):
                def stage(k):
                    if part == 0:
                        pe.wait_ge(S["ones_ok"], 1)
                        pe.wait_ge(S["gelu_ok"], FB * (k + 1))
                        take_side(1, "f2_read", k + 1)
                    for t in range(2 * part, 2 * part + 2):
                        mm(side[1][:, t * D:(t + 1) * D], ones[:], b2row[:], start=True, stop=False)
                        for f in range(FB):
                            ins = mm(side[1][:, t * D:(t + 1) * D], m_t[:, f, t * P:(t + 1) * P], w_m2[:, f, :],
                                     start=False, stop=(f == FB - 1))
                    ins.then_inc(S["f2_mm"], 1)
                return stage

            def hm_to_channels(k):
                pe.wait_ge(S["hm_ok"], k + 1)
                to_channels(take_side(1, "hm_t_ok", k + 1), pay[:, chunk(k), 0:D], S["hm_tr"])

            def gate_logits(k):
                pe.wait_ge(S["hm_t_ok"], k + 1)
                bank = take_side(1, "lg_ok", k + 1)
                for t in range(TC):
                    ins = mm(bank[:, t * NE:(t + 1) * NE], h_t[:, 2, t * P:(t + 1) * P], w_g[:], start=True, stop=True)
                ins.then_inc(S["lg_mm"], 1)

            def bcast_b(k):
                c, n = divmod(k, STEPS)
                if n == 0:
                    pe.wait_ge(S["dbc_ok"], c + 1)
                if k:
                    pe.wait_ge(S["b_copied"], k)
                mm(bank_b, sel[:, n, :], dbc_parts[:, c % 2, :], start=True, stop=True).then_inc(S["b_bcast"], 1)

            def bcast_c(k):
                c, n = divmod(k, STEPS)
                if k:
                    pe.wait_ge(S["weighted"], k)
                mm(bank_c, sel[:, NS + n, :], dbc_parts[:, c % 2, :], start=True, stop=True).then_inc(S["c_bcast"], 1)

            def sum_step(k):
                c, n = divmod(k, STEPS)
                pe.wait_ge(S["weighted"], k + 1)
                if c and n == 0:
                    pe.wait_ge(S["y_read"], c)
                for j in range(NH):
                    ins = mm(ysum[:, j, :], ident, part[:, n % 2, j * CH:(j + 1) * CH], start=(n == 0), stop=(n == STEPS - 1),
                             skip_group_check=True)
                ins.then_inc(S["summed"], 1)

            def to_experts(a, b):
                pe.wait_ge(S["parts_ok"], 1 + (a > 0))
                for k, src in enumerate((m_parts, h_parts)):
                    for t in range(a, b):
                        nc.tensor.transpose(expert_rows(k, a)[:, (t - a) * P:(t - a + 1) * P],
                                            src[:, t, :, :].rearrange("p k e -> p (k e)"), id16[:]).then_inc(S["rt_tr"], 1)

            def count_choices(bank, n):
                for t in range(n):
                    ins = mm(ps[0:NE, bank, t:t + 1], h_parts[:, t, 0, :], minus16[:, 1:2], start=True, stop=True)
                ins.then_inc(S["counts_mm"], 1)

            def before(t, bank, which):
                acc = ps[:, bank, t:t + 1]
                ins = mm(acc, hot_t[:, t * P:(t + 1) * P], tiles_before[:, which, t:t + 1], start=True, stop=(t == 0))
                for i in range(t):
                    ins = mm(acc, greater[i][:, (t - i) * P:(t - i + 1) * P], minus16[:, 0:1], start=False, stop=(i == t - 1))
                ins.then_inc(S["before_mm"], 1)

            def values(q):
                t, i, j = units[q]
                if q >= 5:
                    pe.wait_ge(S["compared"], q - 4)
                mm(unit_bank(q, (j - i) * P), h_rows[:, t * P:(t + 1) * P], m_rows[:, i * P:j * P], start=True, stop=True
                   ).then_inc(S["row_mm"], 1)

            def early_transposes(k):
                pe.wait_ge(S["y_read"], NC)
                to_experts(0, EARLY)
                count_choices(4, EARLY)

            def last_transposes(k):
                to_experts(EARLY, NT)

            def early_before(k):
                if k == 0:
                    pe.wait_ge(S["hot_t_ok"], 1)
                    pe.wait_ge(S["prefix_ok"], 1)
                per = EARLY // 4
                for t in range(per * k, per * k + per):
                    if t:
                        pe.wait_ge(S["compared"], sum(u[0] < t for u in unit_a))
                    before(t, 4, 0)

            def early_values(k):
                if k == 0:
                    pe.wait_ge(S["h_rows_ok"], 1)
                    pe.wait_ge(S["m_rows_ok"], 1)
                for q, (t, i, j) in enumerate(unit_a):
                    if t // (EARLY // 4) == k:
                        values(q)

            beside = BESIDE(("R_TR_T", early_transposes), ("R_VAL_T", early_values),
                            ("R_TR2_T", last_transposes), ("R_BEF_T", early_before), ("MB_T", more_modulation), ("TR_T", hn_to_channels), ("XM0_T", in_proj_x(0)), ("XM1_T", in_proj_x(1)),
                            ("Z0_T", in_proj_z(0)), ("Z1_T", in_proj_z(1)), ("XP_T", x_proj), ("DT0_T", dt_proj(0)),
                            ("DT1_T", dt_proj(1)), ("OP0_T", out_proj(0)), ("OP1_T", out_proj(1)),
                            ("TR2_T", hn2_to_channels), ("UP0_T", mlp_up(0)), ("UP1_T", mlp_up(1)), ("UP2_T", mlp_up(2)),
                            ("UP3_T", mlp_up(3)), ("DOWN0_T", mlp_down(0)), ("DOWN1_T", mlp_down(1)),
                            ("TR3_T", hm_to_channels), ("LG_T", gate_logits))
            beside(-99, -1)
            pe.wait_ge(S["sel_ok"], 1)
            pe.wait_ge(S["mod_bc_copied"], 2 * NB)
            for k in range(B_SENT):
                bcast_b(k)
                if k == 0:
                    bcast_c(0)
            for k in range(NC * STEPS):
                if k + 1 < NC * STEPS:
                    bcast_c(k + 1)
                if k + B_SENT < NC * STEPS:
                    bcast_b(k + B_SENT)
                sum_step(k)
                beside(k, k)
            beside(NC * STEPS, 999)

            pe.wait_ge(S["h_rows_ok"], 2)
            pe.wait_ge(S["m_rows_ok"], 2)
            count_choices(7, NT)
            for q in range(len(unit_a), len(units)):
                values(q)
            pe.wait_ge(S["prefix_ok"], 2)
            pe.wait_ge(S["hot_t_ok"], 2)
            for t in range(EARLY, NT):
                pe.wait_ge(S["compared"], last_unit(t - 1))
                before(t, 7, 1)

            pe.wait_ge(S["ld_e"], 32)
            pe.wait_ge(S["compared"], len(units))
            pe.wait_ge(S["rank_ok"], 2)
            for g in range(ST // 4):
                pe.wait_ge(S["xe_hm"][g], 16)
                if g >= 2:
                    pe.wait_ge(S["xt_ok"], g - 1)
                for s in range(4):
                    ins = nc.tensor.transpose(ps[:, g % 2, s * P:(s + 1) * P], xe[:, 4 * g + s, 0:D], ident)
                ins.then_inc(S["xt_tr"], 1)

            def up(e):
                pe.wait_ge(S["xt_ok"], -(-(e + 1) * CAP // CH))
                if e >= 2:
                    pe.wait_ge(S["e1_ok"], 2 * (e - 1))
                for j in range(2):
                    ins = mm(ps[:, 2 + e % 2, j * CAP:(j + 1) * CAP], w_e1[:, e, j * P:(j + 1) * P],
                             xe_t[:, e * CAP:(e + 1) * CAP], start=True, stop=True)
                ins.then_inc(S["e1_mm"], 1)

            def down(e):
                pe.wait_ge(S["e1_ok"], 2 * (e + 1))
                if e >= 2:
                    pe.wait_ge(S["e2_ok"], e - 1)
                for j in range(2):
                    ins = mm(ps[:, 4 + e % 2, 0:CAP], w_e2[:, e, j, :], g_t[:, e % 2, j, :], start=(j == 0), stop=(j == 1))
                ins.then_inc(S["e2_mm"], 1)

            def to_slots(g):
                a, b = OUT[g]
                pe.wait_ge(S["e2_ok"], -(-b * P // CAP))
                if g >= 2:
                    pe.wait_ge(S["fin_ok"], g - 1)
                for s in range(a, b):
                    ins = nc.tensor.transpose(ps[:, 6 + g % 2, (s - a) * P:(s - a + 1) * P], o_t[:, s * P:(s + 1) * P], ident)
                ins.then_inc(S["o_tr"], 1)

            up(0)
            g = 0
            for e in range(NE):
                if e + 1 < NE:
                    up(e + 1)
                down(e)
                while OUT[g][1] * P <= e * CAP:
                    to_slots(g)
                    g += 1
            while g < len(OUT):
                to_slots(g)
                g += 1


def kernel(**inputs):
    import numpy as np
    import concourse.bacc as bacc
    from concourse.bass_utils import run_bass_kernel_spmd as run

    def arr(n):
        return np.asarray(inputs["L0_" + n])

    def lay(v):
        return np.ascontiguousarray(v)

    def by_part(v, parts):
        return lay(v.reshape(parts, P, -1).transpose(1, 0, 2))

    f = np.float32
    consts = np.zeros((P, 3 * P + 2 * NS + 64), f)
    consts[:, 0:P] = np.eye(P)
    consts[:, P:2 * P] = np.tril(np.ones((P, P)), -1)
    consts[:, 2 * P:2 * P + NT] = np.arange(P)[:, None] + P * np.arange(NT)[None, :] + 1
    consts[:, 2 * P + NT:2 * P + NT + NE] = NE - np.arange(NE)[None, :]
    o = 2 * P + NT + NE
    for k in range(PARTS):
        for n in range(2 * NS):
            consts[k * G + RANK + n, o + n] = 1
        for b in range(NB):
            consts[k * NB + b, o + 2 * NS + b] = 1
    o += 2 * NS + NB
    consts[G:PARTS * G, o] = -1
    consts[2 * G:PARTS * G, o + 1] = -1
    consts[NB:PARTS * NB, o + 2] = -1
    consts[2 * NB:PARTS * NB, o + 3] = -1
    consts[:, o + 4:o + 4 + TC] = -0.5

    x_proj = arr("attn_x_proj_w").T
    chan = np.concatenate([arr("attn_conv_w")[:, 0, :], arr("attn_conv_b")[:, None], arr("attn_dt_proj_b")[:, None],
                           arr("attn_D")[:, None], arr("attn_A_log")], 1)
    cols = np.concatenate([arr("attn_norm1_w")[:, None], arr("attn_norm2_w")[:, None],
                           arr("attn_mlp_b1").reshape(FB, P).T, arr("ffn_b1").reshape(NE * 2, P).T,
                           arr("ffn_b2").T], 1)
    arrays = {
        "x": lay(arr("attn_x").reshape(NT, P, D).transpose(1, 0, 2)),
        "c_t": lay(np.concatenate([arr("c").T] * PARTS, 1)),
        "w_mod": lay(arr("wmod")),
        "consts": consts,
        "cols": lay(cols),
        "chan": by_part(chan, NH),
        "w_in": lay(arr("attn_in_proj_w").T),
        "w_xp": by_part(np.concatenate([x_proj] * PARTS, 1), NH),
        "w_dt": lay(arr("attn_dt_proj_w").T),
        "w_out": by_part(arr("attn_out_proj_w").T, NH),
        "w_m1": lay(arr("attn_mlp_w1").T),
        "w_m2": by_part(arr("attn_mlp_w2").T, FB),
        "b2row": lay(arr("attn_mlp_b2")[None, :]),
        "w_g": lay(arr("ffn_Wg")),
        "w_e1": lay(arr("ffn_W1").transpose(1, 0, 2)),
        "w_e2": lay(arr("ffn_W2").reshape(NE, H // P, P, D).transpose(2, 0, 1, 3)),
    }
    nc = bacc.Bacc("TRN2", target_bir_lowering=False, num_devices=1)
    a = {n: nc.dram_tensor("in_" + n, v.shape, F32, kind="ExternalInput").ap() for n, v in arrays.items()}
    out = nc.dram_tensor("out_0", (NB, T, D), F32, kind="ExternalOutput").ap()
    xe_dram = nc.dram_tensor("xe_rows", (SLOTS, W_PAY), F32, kind="Internal").ap()
    adaln_mamba_moe(nc, a, out, xe_dram)
    r = run(nc, [{"in_" + n: v for n, v in arrays.items()}], core_ids=[0])
    return r.results[0]["out_0"]
```
